# Optimizing a Trainium2 kernel written in Bass

```python
import numpy as np
import jax
import jax.numpy as jnp

def _softmax(x, axis=-1):
    return jax.nn.softmax(x, axis=axis)

def _gelu(x):
    return jax.nn.gelu(x, approximate=True)

def _silu(x):
    return jax.nn.silu(x)

def _sigmoid(x):
    return jax.nn.sigmoid(x)

def _layernorm(x, axis=-1, eps=1e-05):
    m = jnp.mean(x, axis=axis, keepdims=True)
    v = jnp.var(x, axis=axis, keepdims=True)
    return (x - m) / jnp.sqrt(v + eps)

def _scatter_add(tgt, idx, src, axis=0):
    return tgt.at[idx].add(src)

def _segment_sum(src, seg, n):
    return jax.ops.segment_sum(src, seg, n)
kernel_name = 'mk_lm_tower_d1_tok_ids1024_r4_8044fd'

def setup_inputs(seed: int=0):
    np.random.seed(seed)
    _w = jnp.asarray

    def _rec_inputs():
        import jax
        import jax.numpy as jnp
        _rk = jax.random.key(seed)
        x = jax.random.randint(jax.random.fold_in(_rk, 1), (32, 512), 0, 12564, jnp.int32)
        return x
    x = _rec_inputs()

    def _L0_tok_setup():
        import jax, jax.numpy as jnp
        import numpy as np
        VOCAB = 50257
        HIDDEN = 256
        BATCH = 4
        SEQ = 1024
        key = jax.random.key(seed)
        k_idx, k_w = jax.random.split(key)
        idx = jax.random.randint(k_idx, (BATCH, SEQ), 0, VOCAB, dtype=jnp.int64 if jax.config.jax_enable_x64 else jnp.int32)
        weight = jax.random.normal(k_w, (VOCAB, HIDDEN), dtype=jnp.float32)
        return {'idx': idx, 'weight': weight}
    _L0_tok_all = _L0_tok_setup()
    _L0_tok_in = {k: v for k, v in _L0_tok_all.items() if k in ('weight',)}
    del _L0_tok_all

    def _L0_attn_setup():
        import math
        import jax, jax.numpy as jnp
        import numpy as np
        B, T, C = (2, 512, 256)
        H = 16
        D = C // H

        def alibi_slopes(n_heads):

            def pow2_slopes(n):
                start = 2.0 ** (-2.0 ** (-(math.log2(n) - 3)))
                return [start * start ** i for i in range(n)]
            if n_heads & n_heads - 1 == 0:
                s = pow2_slopes(n_heads)
            else:
                cp2 = 2 ** math.floor(math.log2(n_heads))
                s = pow2_slopes(cp2)
                extra_base = 2.0 ** (-2.0 ** (-(math.log2(2 * cp2) - 3)))
                s.extend([extra_base * extra_base ** i for i in range(n_heads - cp2)])
                s = s[:n_heads]
            return jnp.asarray(s, dtype=jnp.float32)
        key = jax.random.key(seed)
        k1, k2, k3 = jax.random.split(key, 3)
        x = jax.random.normal(k1, (B, T, C), dtype=jnp.float32)
        W_attn = jax.random.normal(k2, (3 * C, C), dtype=jnp.float32) * 0.02
        W_proj = jax.random.normal(k3, (C, C), dtype=jnp.float32) * 0.02
        return {'x': x, 'W_attn': W_attn, 'W_proj': W_proj}
    _L0_attn_all = _L0_attn_setup()
    _L0_attn_in = {k: v for k, v in _L0_attn_all.items() if k in ('W_attn', 'W_proj')}
    del _L0_attn_all

    def _L0_ffn_setup():
        import jax, jax.numpy as jnp
        import numpy as np
        EPS = 1e-05

        def _quantize(W):
            gamma = jnp.mean(jnp.abs(W))
            return jnp.clip(jnp.round(W / (gamma + EPS)), -1.0, 1.0)
        key = jax.random.key(seed)
        k_x, k_w1, k_b1, k_w2, k_b2 = jax.random.split(key, 5)
        n_embd = 256
        d_ff = 4 * n_embd
        B, S = (4, 1024)
        bound1 = 1.0 / np.sqrt(n_embd)
        bound2 = 1.0 / np.sqrt(d_ff)
        x = jax.random.normal(k_x, (B, S, n_embd), dtype=jnp.float32)
        W1 = jax.random.uniform(k_w1, (d_ff, n_embd), jnp.float32, -bound1, bound1)
        b1 = jax.random.uniform(k_b1, (d_ff,), jnp.float32, -bound1, bound1)
        W2 = jax.random.uniform(k_w2, (n_embd, d_ff), jnp.float32, -bound2, bound2)
        b2 = jax.random.uniform(k_b2, (n_embd,), jnp.float32, -bound2, bound2)
        return {'x': x, 'W1': W1, 'b1': b1, 'W2': W2, 'b2': b2}
    _L0_ffn_all = _L0_ffn_setup()
    _L0_ffn_in = {k: v for k, v in _L0_ffn_all.items() if k in ('W1', 'b1', 'W2', 'b2')}
    del _L0_ffn_all
    return {'x': x, 'L0_tok_weight': _L0_tok_in['weight'], 'L0_attn_W_attn': _L0_attn_in['W_attn'], 'L0_attn_W_proj': _L0_attn_in['W_proj'], 'L0_ffn_W1': _L0_ffn_in['W1'], 'L0_ffn_b1': _L0_ffn_in['b1'], 'L0_ffn_W2': _L0_ffn_in['W2'], 'L0_ffn_b2': _L0_ffn_in['b2']}

def reference(x, L0_tok_weight, L0_attn_W_attn, L0_attn_W_proj, L0_ffn_W1, L0_ffn_b1, L0_ffn_W2, L0_ffn_b2):
    import jax
    import jax.numpy as jnp

    def _L0_tok_ref(idx, weight):
        import jax, jax.numpy as jnp
        import numpy as np
        VOCAB = 50257
        HIDDEN = 256
        BATCH = 4
        SEQ = 1024
        return jnp.take(weight, idx, axis=0)

    def _L0_attn_ref(x, W_attn, W_proj):
        import math
        import jax, jax.numpy as jnp
        import numpy as np
        B, T, C = (2, 512, 256)
        H = 16
        D = C // H

        def alibi_slopes(n_heads):

            def pow2_slopes(n):
                start = 2.0 ** (-2.0 ** (-(math.log2(n) - 3)))
                return [start * start ** i for i in range(n)]
            if n_heads & n_heads - 1 == 0:
                s = pow2_slopes(n_heads)
            else:
                cp2 = 2 ** math.floor(math.log2(n_heads))
                s = pow2_slopes(cp2)
                extra_base = 2.0 ** (-2.0 ** (-(math.log2(2 * cp2) - 3)))
                s.extend([extra_base * extra_base ** i for i in range(n_heads - cp2)])
                s = s[:n_heads]
            return jnp.asarray(s, dtype=jnp.float32)
        b, t, c = x.shape
        slopes = alibi_slopes(H)
        qkv = jnp.einsum('btc,fc->btf', x, W_attn)
        q, k, v = jnp.split(qkv, 3, axis=-1)
        q = q.reshape(b, t, H, D).transpose(0, 2, 1, 3)
        k = k.reshape(b, t, H, D).transpose(0, 2, 1, 3)
        v = v.reshape(b, t, H, D).transpose(0, 2, 1, 3)
        scale = 1.0 / math.sqrt(D)
        scores = jnp.einsum('bhqd,bhkd->bhqk', q, k) * scale
        pos = jnp.arange(t, dtype=jnp.float32)
        rel = pos[None, :] - pos[:, None]
        causal = pos[None, :] <= pos[:, None]
        bias = slopes[:, None, None] * rel[None, :, :]
        bias = jnp.where(causal[None, :, :], bias, -jnp.inf)
        scores = scores + bias[None]
        att = jax.nn.softmax(scores, axis=-1)
        y = jnp.einsum('bhqk,bhkd->bhqd', att, v)
        y = y.transpose(0, 2, 1, 3).reshape(b, t, c)
        y = jnp.einsum('btc,oc->bto', y, W_proj)
        return y

    def _L0_ffn_ref(x, W1, b1, W2, b2):
        import jax, jax.numpy as jnp
        import numpy as np
        EPS = 1e-05

        def _quantize(W):
            gamma = jnp.mean(jnp.abs(W))
            return jnp.clip(jnp.round(W / (gamma + EPS)), -1.0, 1.0)
        Wq1 = _quantize(W1)
        Wq2 = _quantize(W2)
        h = jax.nn.relu(jnp.einsum('bsd,fd->bsf', x, Wq1) + b1)
        out = jnp.einsum('bsf,df->bsd', h, Wq2) + b2
        return out
    h = _L0_tok_ref(x, L0_tok_weight)
    h = h + _L0_attn_ref(_layernorm(h, axis=-1), L0_attn_W_attn, L0_attn_W_proj)
    h = h + _L0_ffn_ref(_layernorm(h, axis=-1), L0_ffn_W1, L0_ffn_b1, L0_ffn_W2, L0_ffn_b2)
    return h

_drawn_inputs = setup_inputs


def setup_inputs(seed=0):
    import zlib

    import numpy as np

    out = dict(_drawn_inputs(seed))
    spreads = {}
    factors = {'L0_ffn_b1': 21.992, 'L0_ffn_b2': 64.0}
    for name, (base, spread) in spreads.items():
        noise = np.random.default_rng([zlib.crc32(name.encode()), seed]).standard_normal(out[name].shape)
        drawn = base * np.exp(spread * noise) if base else spread * noise
        out[name] = jnp.asarray(drawn.astype(out[name].dtype))
    for name, factor in factors.items():
        out[name] = (out[name] * factor).astype(out[name].dtype)
    return out
```

```python
from contextlib import ExitStack

import numpy as np

import concourse.bass as bass
from concourse import mybir

F32 = mybir.dt.float32
F32R = mybir.dt.float32r
BF16 = mybir.dt.bfloat16
I32 = mybir.dt.int32
ACT = mybir.ActivationFunctionType
ALU = mybir.AluOpType
AX = mybir.AxisListType

P = 128
NB, T, C, FF = 32, 512, 256, 1024
H, D = 16, 16
NT = T // P
CC = C // P
FC = FF // P
GROUPS, GH = 4, 4
UNITS = 10
SLOTS = GROUPS * UNITS
LEAD = 15
EPS = 1e-5
MASKED = -1.0e38
ALIBI_ROWS = 6
PART_ROWS = 6 * D
MAX_ROW = ALIBI_ROWS + PART_ROWS
K_SCORES = MAX_ROW
K_SHIFTED = MAX_ROW + 3
SUB = 16
SUB_ROWS = P // SUB - 1
K_DIAGONAL = K_SHIFTED + SUB_ROWS
Q_SPREAD = [(0, 3, 0, 0), (3, 2, 1, 1), (5, 1, 1, 1)]
K_SPREAD = [(0, 3, 0, 1), (3, 2, 0, 0), (5, 1, 1, 1)]


class Batch:

    def __init__(self, reg, off=0):
        self.reg, self.off = reg, off

    def __add__(self, n):
        return Batch(self.reg, self.off + n)

    def __sub__(self, n):
        return Batch(self.reg, self.off - n)

    def times(self, n, more=0):
        return self.reg * n + (self.off * n + more)


def present(b):
    return isinstance(b, Batch) or 0 <= b < NB


def wait(eng, sem, per, b, n):
    if isinstance(b, Batch):
        eng.wait_ge(sem, b.times(per, n))
    elif 0 <= b < NB and b * per + n > 0:
        eng.wait_ge(sem, b * per + n)


def row(b, scale=1):
    return b.times(scale) if isinstance(b, Batch) else b * scale


def s_blocks(n):
    if n < 4:
        return [(n, 3, 0)]
    if n < 8:
        return [(n - 4, 2, 0), (n - 4, 0, 384)]
    return [(2 * (n - 8), 1, 0), (2 * (n - 8) + 1, 1, 256)]


def st_blocks(n):
    if n < 4:
        return [(n, 0, 0)]
    if n < 8:
        return [(n - 4, 1, 0), (n - 4, 3, 384)]
    return [(2 * (n - 8), 2, 0), (2 * (n - 8) + 1, 2, 256)]


P_AT = {(h, kb): (n, col) for n in range(UNITS) for h, kb, col in st_blocks(n)}

XT_SLOT = {0: 0, 2: 1}
QK_SLOT = {6: 0, 9: 1, 12: 2, 16: 3}
V_SLOT = {19: 0, 22: 1}
MAX_SLOT = {5: 1, 15: 2, 25: 3, 35: 4}
PROJ_SLOT = {12: 0, 14: 1}
X2T_SLOT = {17: 0, 20: 1}
F1_SLOT = {19: 0, 21: 1, 23: 2, 25: 3, 27: 4, 29: 5, 31: 6, 33: 7}
F2_SLOT = {24: 0, 26: 1, 28: 2, 30: 3, 32: 4, 34: 5, 36: 6, 38: 7}
PV_SLOT = {6: 0, 0: 1, 2: 2}

FRONT_USES = sorted([(s, "xt", n) for s, n in XT_SLOT.items()] + [(s, "qk", n) for s, n in QK_SLOT.items()]
                    + [(s, "v", n) for s, n in V_SLOT.items()] + [(s, "max", n) for s, n in MAX_SLOT.items()])


def front_batch(kind, n, t):
    return t if kind == "max" and n < 4 else t + 1


def block_program(nc, x, table, w_attn, w_proj, w1, b1, w2, b2, q_const, k_const, out):
    with ExitStack() as ctx:
        def sb(name, shape, dt):
            return ctx.enter_context(nc.sbuf_tensor(name, shape, dt))

        def bank(name):
            return ctx.enter_context(nc.psum_tensor(name, [P, 512], F32))

        def sem(name):
            return ctx.enter_context(nc.semaphore(name))

        ids = sb("ids", [P, NT], I32)
        emb = sb("emb", [P, 2, NT, C], F32)
        res = sb("res", [P, 2, NT, C], F32)
        xn = sb("xn", [P, NT, C], F32)
        xT_hi = sb("xT_hi", [P, CC, T], F32R)
        xT_lo = sb("xT_lo", [P, CC, T], F32R)
        x2T_hi = sb("x2T_hi", [P, CC, T], F32R)
        x2T_lo = sb("x2T_lo", [P, CC, T], F32R)
        parts = sb("parts", [P, 2, 3, T], BF16)
        qk_rest = sb("qk_rest", [P, T], F32)
        q_aug = sb("q_aug", [P, 2, H, T], BF16)
        k_aug = sb("k_aug", [P, 2, H, T], BF16)
        v_aug = sb("v_aug", [P, 2, NT, H, 2 * D], F32)
        prob = sb("prob", [P, UNITS, T], F32)
        y_raw = sb("y_raw", [P, T], F32)
        yT = sb("yT", [P, CC, T], F32)
        denom = sb("denom", [P, T], F32)
        h_full = sb("h_full", [P, 2, 2, 256], F32)
        h_hi = sb("h_hi", [P, FC, 256], F32R)
        h_lo = sb("h_lo", [P, FC, 256], F32R)
        wqk_hi = sb("wqk_hi", [P, CC, 4, P], F32R)
        wqk_lo = sb("wqk_lo", [P, CC, 4, P], F32R)
        wv_hi = sb("wv_hi", [P, CC, C], F32R)
        wv_lo = sb("wv_lo", [P, CC, C], F32R)
        wp = sb("wp", [P, CC, C], F32)
        w1T = sb("w1T", [P, CC, FF], F32R)
        w2T = sb("w2T", [P, FC, C], F32R)
        b1_col = sb("b1_col", [P, FC], F32)
        b2_row = sb("b2_row", [P, C], F32)
        ident = sb("ident", [P, P], F32)
        mask = sb("mask", [P, T], BF16)
        row_max = sb("row_max", [P, 2, 16], F32)
        m_parts = sb("m_parts", [16, 3, P], BF16)
        m_rest = sb("m_rest", [16, P], F32)
        stats = sb("stats", [P, 2, NT, 6], F32)
        mean_var = sb("mean_var", [P, 2, NT, 2], F32)
        rstd = sb("rstd", [P, 2, NT], F32)
        neg_half = sb("neg_half", [P, NT], F32)
        w_sum = sb("w_sum", [P, 2], F32)
        w_thr = sb("w_thr", [P, 4], F32)
        ones = qk_rest[:, 0:P]
        raw_attn = prob[:, 0:3, :].rearrange("p a b -> p (a b)").rearrange("p (j c) -> p j c", c=C)
        raw_proj = prob[:, 3, :].rearrange("p (j c) -> p j c", c=C)
        raw_w1 = prob[:, 4:8, :].rearrange("p a b -> p (a b)")
        raw_w2 = res[:].rearrange("p a b c -> p (a b c)")
        neg_w1 = q_aug[:, 0, :, :].rearrange("p a b -> p (a b)")[:, 0:2 * FC * C].bitcast(F32)

        s_bank = [bank("s_bank0"), bank("s_bank1")]
        st_bank = [bank("st_bank0"), bank("st_bank1")]
        pv_bank = bank("pv_bank")
        front_bank = bank("front_bank")
        ffn_bank = bank("ffn_bank")
        acc_bank = bank("acc_bank")

        scratch = nc.dram_tensor("parts_scratch", [4, 3, P, T], BF16, kind="Internal").ap()

        w_in = sem("w_in")
        const_ok = sem("const_ok")
        aug_const_in = sem("aug_const_in")
        w_step = sem("w_step")
        w_mm = sem("w_mm")
        w_ready = sem("w_ready")
        ids_in = sem("ids_in")
        emb_in = sem("emb_in")
        res_in = sem("res_in")
        ln_step = [sem("ln1_step"), sem("ln2_step")]
        rstd_step = [sem("rstd1_step"), sem("rstd2_step")]
        ln1_done = sem("ln1_done")
        xt_mm, xt_hi, xt_lo = sem("xt_mm"), sem("xt_hi"), sem("xt_lo")
        qk_mm, qk_hi, qk_r = sem("qk_mm"), sem("qk_hi"), sem("qk_r")
        qk_mid, qk_lo = sem("qk_mid"), sem("qk_lo")
        scratch_w = sem("scratch_w")
        aug_in = [sem(f"aug_in{n}") for n in range(4)]
        v_mm, v_ev = sem("v_mm"), sem("v_ev")
        s_mm, s_max = sem("s_mm"), sem("s_max")
        m_mm, m_step = sem("m_mm"), sem("m_step")
        m_in = [sem(f"m_in{g}") for g in range(GROUPS)]
        st_mm, exp_done, zero_done = sem("st_mm"), sem("exp_done"), sem("zero_done")
        pv_mm, y_ev = sem("pv_mm"), sem("y_ev")
        y_in = [sem(f"y_in{g}") for g in range(GROUPS)]
        y_rec, y_nrm = sem("y_rec"), sem("y_nrm")
        pr_mm, res_add = sem("pr_mm"), sem("res_add")
        ln2_done = sem("ln2_done")
        x2t_mm, x2t_hi, x2t_lo = sem("x2t_mm"), sem("x2t_hi"), sem("x2t_lo")
        f1_mm, f1_relu, f1_hi, f1_lo = sem("f1_mm"), sem("f1_relu"), sem("f1_hi"), sem("f1_lo")
        f2_mm, out_add = sem("f2_mm"), sem("out_add")
        b2_add = sem("b2_add")
        out_w = sem("out_w")

        block = ctx.enter_context(nc.Block())

        def wait_alone(eng, sem, per, b, n):
            wait(eng, sem, per, b, n)
            if isinstance(b, Batch):
                eng.nop(nofuse=True)

        def schedule(eng, iteration):
            for t in (-1, 0, 1):
                iteration(t, t % 2)
            with eng.Fori(2, NB - 3, 2) as t:
                iteration(Batch(t), 0)
                iteration(Batch(t, 1), 1)
            for t in (NB - 2, NB - 1, NB):
                iteration(t, t % 2)

        def score_unit(t, slot):
            u = slot + LEAD
            return (t, u) if u < SLOTS else (t + 1, u - SLOTS)

        @block.sync
        def _(sp):
            with nc.allow_non_contiguous_dma(reason="small columns"):
                sp.dma_start(raw_attn, w_attn.rearrange("(j p) c -> p j c", p=P)).then_inc(w_in, 16)
                sp.dma_start(raw_proj, w_proj.rearrange("(j p) c -> p j c", p=P)).then_inc(w_in, 16)
                sp.dma_start(raw_w1.rearrange("p (j c) -> p j c", c=C),
                             w1.rearrange("(j p) c -> p j c", p=P)).then_inc(w_in, 16)
                sp.dma_start(raw_w2.rearrange("p (j c) -> p j c", c=FF),
                             w2.rearrange("(j p) c -> p j c", p=P)).then_inc(w_in, 16)
                sp.dma_start(b1_col[:], b1.rearrange("(j p) -> p j", p=P)).then_inc(w_in, 16)
                sp.dma_start(b2_row[:], b2.rearrange("(a c) -> a c", a=1).to_broadcast([P, C])).then_inc(w_in, 16)
            sp.wait_ge(w_ready, 1)
            for par in range(2):
                sp.dma_start(q_aug[0:ALIBI_ROWS, par, :, :].rearrange("p h t -> p (h t)"),
                             q_const[0:ALIBI_ROWS, :]).then_inc(aug_const_in, 16)
                sp.dma_start(k_aug[0:ALIBI_ROWS, par, :, :].rearrange("p h t -> p (h t)"),
                             k_const[0:ALIBI_ROWS, :]).then_inc(aug_const_in, 16)
                sp.dma_start(q_aug[K_SHIFTED:K_DIAGONAL, par, :, :].rearrange("p h t -> p (h t)"),
                             q_const[ALIBI_ROWS:, :]).then_inc(aug_const_in, 16)
                sp.dma_start(k_aug[MAX_ROW:K_DIAGONAL, par, :, :].rearrange("p h t -> p (h t)"),
                             k_const[ALIBI_ROWS:, :]).then_inc(aug_const_in, 16)

            def load_ids(b):
                wait_alone(sp, emb_in, 64, b - 1, 64)
                with nc.allow_non_contiguous_dma(reason="2 KB of ids"):
                    src = x[bass.ds(row(b), 1), :].rearrange("o (j p) -> p (o j)", p=P)
                    sp.dma_start(ids[:], src).then_inc(ids_in, 16)

            def spread(b, par, n):
                aug, plan = (q_aug, Q_SPREAD) if n % 2 == 0 else (k_aug, K_SPREAD)
                h0 = 8 * (n // 2)
                wait_alone(sp, qk_lo, 4, b, n + 1)
                wait_alone(sp, aug_in[n], 48, b - 1, 48)
                sp.dma_start(scratch[n].rearrange("a p t -> p a t"), parts[:, n % 2, :, :]).then_inc(scratch_w, 16)
                wait_alone(sp, scratch_w, 64, b, 16 * n + 16)
                wait_alone(sp, st_mm, 40, b - 2, 40)
                for g0, count, part, step in plan:
                    for_part = scratch[n, part:part + (count if step else 1)]
                    src = for_part.rearrange("a (d h) t -> a d (h t)", h=8)
                    if not step and count > 1:
                        src = src.to_broadcast([count, D, 8 * T])
                    r0 = ALIBI_ROWS + g0 * D
                    dst = aug[r0:r0 + count * D, par, h0:h0 + 8, :].rearrange("p h t -> p (h t)")
                    sp.dma_start(dst, src).then_inc(aug_in[n], 16)

            def iteration(t, par):
                for slot in range(SLOTS):
                    if slot == 0 and present(t):
                        wait_alone(sp, out_w, 16, t - 2, 16)
                        wait_alone(sp, emb_in, 64, t, 64)
                        if not isinstance(t, Batch) and t < 2:
                            sp.wait_ge(w_ready, 1)
                        sp.dma_start(res[:, par], emb[:, par]).then_inc(res_in, 16)
                        if present(t + 2):
                            load_ids(t + 2)
                    if slot == 0 and isinstance(t, int) and t == -1:
                        load_ids(0)
                        load_ids(1)
                    if slot in (8, 11, 14, 18) and present(t + 1):
                        spread(t + 1, 1 - par, (8, 11, 14, 18).index(slot))
                    if slot in (7, 17, 27, 37):
                        g = (slot + 3) // 10
                        b, bp = (t, par) if g < 4 else (t + 1, 1 - par)
                        g %= 4
                        if present(b):
                            wait_alone(sp, m_step, 16, b, 4 * g + 4)
                            wait_alone(sp, st_mm, 40, b - 2, 40)
                            for k in range(3):
                                dst = q_aug[MAX_ROW + k:MAX_ROW + k + 1, bp, GH * g:GH * g + GH, :]
                                sp.dma_start(dst.rearrange("p h t -> p (h t)"),
                                             m_parts[:, k, :]).then_inc(m_in[g], 16)
                    if slot in (4, 14, 24, 34):
                        g = slot // 10 - 1
                        b = t if g >= 0 else t - 1
                        g %= 4
                        if present(b):
                            wait_alone(sp, y_ev, 4, b, g + 1)
                            wait_alone(sp, pr_mm, 2, b - 1, 2)
                            wait_alone(sp, y_nrm, 2, b if g >= 2 else b - 1, 1 if g >= 2 else 2)
                            rows = slice(64 * (g % 2), 64 * (g % 2) + 64)
                            sp.dma_start(yT[rows, g // 2, :], y_raw[0:127:2, :]).then_inc(y_in[g], 16)
                            sp.dma_start(denom[rows, :], y_raw[1:128:2, :]).then_inc(y_in[g], 16)
                    if slot == 39 and present(t - 1):
                        wait_alone(sp, out_add, 2, t - 1, 2)
                        dst = out[bass.ds(row(t - 1, T), T), :].rearrange("(j p) c -> p j c", p=P)
                        sp.dma_start(dst, res[:, 1 - par]).then_inc(out_w, 16)

            schedule(sp, iteration)
            sp.wait_ge(out_w, 16 * NB)

        @block.gpsimd
        def _(pool):
            pool.memset(ident[:], 0.0).then_inc(const_ok, 1)
            pool.memset(ones, 1.0).then_inc(const_ok, 1)
            pool.memset(mask[:], 0.0).then_inc(const_ok, 1)
            pool.memset(v_aug[:].rearrange("p a b c d -> p (a b c d)"), 1.0).then_inc(const_ok, 1)
            pool.memset(neg_half[:], -0.5).then_inc(const_ok, 1)
            pool.wait_ge(const_ok, 5)
            pool.affine_select(out=ident[:], in_=ident[:], compare_op=ALU.not_equal, fill=1.0, base=0,
                               pattern=[[-1, P]], channel_multiplier=1).then_inc(const_ok, 1)
            pool.affine_select(out=mask[:, T - P:T], in_=mask[:, T - P:T], compare_op=ALU.is_ge, fill=MASKED,
                               base=0, pattern=[[-1, P]], channel_multiplier=1).then_inc(const_ok, 1)

            def gather(b, par):
                wait(pool, ids_in, 16, b, 16)
                wait(pool, res_in, 16, b - 2, 16)
                wait_alone(pool, ln1_done, 4, b - 2, 4)
                for j in range(NT):
                    pool.indirect_dma_start(
                        out=emb[:, par, j, :], out_offset=None, in_=table,
                        in_offset=bass.IndirectOffsetOnAxis(ap=ids[:, j:j + 1], axis=0)).then_inc(emb_in, 16)

            def zero_future(b, n):
                wait_alone(pool, exp_done, 40, b, n + 1)
                m = n % UNITS
                if m < 4:
                    v, pat = prob[:, m, 0:P], [[1, P]]
                elif m < 8:
                    v, pat = prob[:, m, :].rearrange("p (a q) -> p a q", q=P)[:, 0:4:3, :], [[0, 2], [1, P]]
                else:
                    v, pat = prob[:, m, :].rearrange("p (a q) -> p a q", q=P)[:, 0:4:2, :], [[0, 2], [1, P]]
                pool.affine_select(out=v, in_=v, compare_op=ALU.is_ge, fill=0.0, base=0,
                                   pattern=pat, channel_multiplier=-1).then_inc(zero_done, 1)

            def qk_low(b, n):
                wait(pool, qk_mid, 4, b, n + 1)
                wait(pool, scratch_w, 64, b if n >= 2 else b - 1, 16 * ((n - 2) % 4) + 16)
                pool.tensor_tensor(parts[:, n % 2, 2, :], qk_rest[:], parts[:, n % 2, 1, :],
                                   ALU.subtract).then_inc(qk_lo, 1)

            def hidden_low(b, n):
                wait(pool, f1_hi, 8, b, n + 1)
                wait(pool, f2_mm, 8, b if n >= 4 else b - 1, (n - 4) % 8 + 1)
                u = n % 4
                pool.tensor_tensor(h_lo[:, 2 * u:2 * u + 2, :], h_full[:, n % 2], h_hi[:, 2 * u:2 * u + 2, :],
                                   ALU.subtract).then_inc(f1_lo, 1)

            def add_b2(b, par, j):
                wait(pool, ln2_done, 4, b, 2 * j + 2)
                for i in range(2):
                    pool.tensor_tensor(res[:, par, 2 * j + i, :], res[:, par, 2 * j + i, :], b2_row[:],
                                       ALU.add).then_inc(b2_add, 1)

            def reciprocal_root(b, which, half):
                t0, t1 = (0, NT) if which == 0 else (2 * half, 2 * half + 2)
                wait_alone(pool, ln_step[which], 2 * NT, b, 2 * NT if which == 0 else 4 * half + 4)
                pool.tensor_scalar(rstd[:, which, t0:t1], mean_var[:, which, t0:t1, 1], EPS, None,
                                   ALU.add).then_inc(rstd_step[which], 1)
                wait(pool, rstd_step[which], 2 + 2 * which, b, 2 * half + 1)
                pool.tensor_tensor(rstd[:, which, t0:t1], rstd[:, which, t0:t1], neg_half[:, t0:t1],
                                   ALU.pow).then_inc(rstd_step[which], 1)

            def iteration(t, par):
                for slot in range(SLOTS):
                    if slot == 0 and isinstance(t, int) and t == -1:
                        gather(0, 0)
                        gather(1, 1)
                        reciprocal_root(0, 0, 0)
                    if slot in (13, 15) and present(t - 1):
                        reciprocal_root(t - 1, 1, (13, 15).index(slot))
                    if slot == 34 and present(t + 2):
                        reciprocal_root(t + 2, 0, 0)
                    if slot == 1 and present(t) and present(t + 2):
                        gather(t + 2, par)
                    if present(t):
                        zero_future(t, slot)
                    if slot in (7, 10, 13, 17) and present(t + 1):
                        qk_low(t + 1, (7, 10, 13, 17).index(slot))
                    if slot in (20, 23) and present(t - 1):
                        add_b2(t - 1, 1 - par, (20, 23).index(slot))
                    if slot in F1_SLOT and present(t - 1):
                        hidden_low(t - 1, F1_SLOT[slot])

            pool.wait_ge(w_in, 96)
            schedule(pool, iteration)

        @block.scalar
        def _(act):
            def split_high(dst, src, mm, done, per, b, n):
                wait(act, mm, per, b, n + 1)
                act.copy(dst, src).then_inc(done, 1)

            def exp_unit(b, n):
                g, m = n // UNITS, n % UNITS
                wait(act, st_mm, 40, b, n + 1)
                part = 1 if m < 4 else 2 if m < 8 else 3
                if m in (0, 4, 8):
                    if g:
                        wait(act, pv_mm, 12, b, 3 * (g - 1) + part)
                    else:
                        wait(act, pv_mm, 12, b - 1, 9 + part)
                act.activation(prob[:, m, :], st_bank[n % 2][:], ACT.Exp).then_inc(exp_done, 1)

            def iteration(t, par):
                for slot in range(SLOTS):
                    if present(t):
                        exp_unit(t, slot)
                    b = t + 1
                    if slot in XT_SLOT and present(b):
                        n = XT_SLOT[slot]
                        wait(act, v_mm, 2, b - 1, 2)
                        split_high(xT_hi[:, n, :], front_bank[:], xt_mm, xt_hi, 2, b, n)
                    if slot in QK_SLOT and present(b):
                        n = QK_SLOT[slot]
                        wait(act, scratch_w, 64, b if n >= 2 else b - 1, 16 * ((n - 2) % 4) + 16)
                        split_high(parts[:, n % 2, 0, :], front_bank[:], qk_mm, qk_hi, 4, b, n)
                    if slot % 10 == 3:
                        g = slot // 10 - 1
                        b = t if g >= 0 else t - 1
                        g %= 4
                        if present(b):
                            wait(act, pv_mm, 12, b, 3 * g + 3)
                            wait(act, y_in[(g - 1) % 4], 32, b if g else b - 1, 32)
                            act.copy(y_raw[:], pv_bank[:]).then_inc(y_ev, 1)
                    b = t - 1
                    if slot in X2T_SLOT and present(b):
                        n = X2T_SLOT[slot]
                        wait(act, f1_mm, 8, b - 1, 4 * n + 4)
                        split_high(x2T_hi[:, :, 256 * n:256 * n + 256],
                                   ffn_bank[:].rearrange("p (c q) -> p c q", c=CC), x2t_mm, x2t_hi, 2, b, n)
                    if slot in F1_SLOT and present(b):
                        n = F1_SLOT[slot]
                        u = n % 4
                        wait(act, f1_mm, 8, b, n + 1)
                        wait(act, f1_lo, 8, b if n >= 2 else b - 1, (n - 2) % 8 + 1)
                        for i in range(2):
                            act.activation(h_full[:, n % 2, i, :], ffn_bank[:, 256 * i:256 * i + 256], ACT.Relu,
                                           bias=b1_col[:, 2 * u + i:2 * u + i + 1]).then_inc(f1_relu, 1)
                        wait(act, f1_relu, 16, b, 2 * n + 2)
                        wait(act, f2_mm, 8, b if n >= 4 else b - 1, (n - 4) % 8 + 1)
                        act.copy(h_hi[:, 2 * u:2 * u + 2, :], h_full[:, n % 2]).then_inc(f1_hi, 1)

            act.wait_ge(w_in, 96)
            act.wait_ge(w_ready, 1)
            schedule(act, iteration)

        @block.vector
        def _(dve):
            steps = [0]

            def link(ins):
                steps[0] += 1
                ins.then_inc(w_step, 1)
                dve.wait_ge(w_step, steps[0])

            dve.wait_ge(w_in, 96)
            for n, raw in enumerate((raw_w1, raw_w2)):
                link(dve.tensor_reduce(w_sum[:, n:n + 1], raw, AX.X, ALU.add, apply_absolute_value=True))
            dve.wait_ge(w_mm, 1)
            link(dve.tensor_scalar(w_thr[:, 0:2], acc_bank[:, 0:2], 1.0 / (FF * C), EPS, ALU.mult, ALU.add))
            link(dve.tensor_scalar(w_thr[:, 2:4], w_thr[:, 0:2], -0.5, None, ALU.mult))
            link(dve.tensor_scalar(w_thr[:, 0:2], w_thr[:, 0:2], 0.5, None, ALU.mult))
            for n, raw in enumerate((raw_w1, raw_w2)):
                link(dve.tensor_scalar(neg_w1, raw, w_thr[:, 2 + n:3 + n], None, ALU.is_lt))
                link(dve.scalar_tensor_tensor(out=raw, in0=raw, scalar=w_thr[:, n:n + 1], in1=neg_w1,
                                              op0=ALU.is_gt, op1=ALU.subtract))
            QUANT = steps[0]
            assert QUANT == W_QUANT_STEPS

            done = 1
            for k in range(FC // 2):
                done += 1
                dve.wait_ge(w_mm, done)
                link(dve.tensor_copy(w1T[:, :, 256 * k:256 * k + 256],
                                     front_bank[:].rearrange("p (c f) -> p c f", c=CC)))
            for k in range(FC // 2):
                done += 1
                dve.wait_ge(w_mm, done)
                link(dve.tensor_copy(w2T[:, 2 * k:2 * k + 2, :],
                                     front_bank[:].rearrange("p (f c) -> p f c", c=C)))
            for k in range(3):
                done += 1
                dve.wait_ge(w_mm, done)
                src = front_bank[:].rearrange("p (c f) -> p c f", c=CC)
                if k == 2:
                    link(dve.tensor_copy(wv_hi[:], src))
                    link(dve.tensor_tensor(wv_lo[:], src, wv_hi[:], ALU.subtract))
                    continue
                scale = D ** -0.5 if k == 0 else 1.0
                for c in range(CC):
                    for half in range(2):
                        s = src[:, c, P * half:P * half + P].rearrange("p (h d) -> p h d", h=8)
                        n = 2 * half + k
                        hi = wqk_hi[:, c, n, :].rearrange("p (d h) -> p h d", h=8)
                        lo = wqk_lo[:, c, n, :].rearrange("p (d h) -> p h d", h=8)
                        link(dve.tensor_scalar(hi, s, scale, None, ALU.mult))
                        link(dve.scalar_tensor_tensor(out=lo, in0=s, scalar=scale, in1=hi, op0=ALU.mult,
                                                      op1=ALU.subtract))
            done += 1
            dve.wait_ge(w_mm, done)
            link(dve.tensor_copy(wp[:], front_bank[:].rearrange("p (c f) -> p c f", c=CC)))
            dve.drain().then_inc(w_ready, 1)

            def max_unit(t, par, slot):
                b, n = score_unit(t, slot)
                if not present(b):
                    return
                g, m = n // UNITS, n % UNITS
                if m == 0:
                    wait(dve, m_mm, 4, b if g >= 2 else b - 1, (g - 2) % 4 + 1)
                wait_alone(dve, s_mm, 40, b, n + 1)
                blocks = s_blocks(m)
                for i, (h, qb, col) in enumerate(blocks):
                    w = (qb + 1) * P
                    bank_cols = s_bank[n % 2][:, col:col + w]
                    ins = dve.tensor_tensor_reduce(bank_cols, bank_cols, mask[:, T - w:T], 1.0, MASKED,
                                                   ALU.add, ALU.max, row_max[:, g % 2, GH * h + qb:GH * h + qb + 1])
                ins.then_inc(s_max, 1)

            def norm_tiles(src, which, tiles, b, base, done):
                step, rs = ln_step[which], rstd_step[which]
                for j in tiles:
                    dve.bn_stats(stats[:, which, j, :], src[:, j, :]).then_inc(step, 1)
                wait_alone(dve, step, 2 * NT, b, base + len(tiles))
                for j in tiles:
                    dve.bn_aggr(mean_var[:, which, j, :], stats[:, which, j, :]).then_inc(step, 1)
                wait(dve, rs, 2 + 2 * which, b, 2 * (base // 4) + 2)
                for j in tiles:
                    dve.tensor_scalar(xn[:, j, :], src[:, j, :], mean_var[:, which, j, 0:1],
                                      rstd[:, which, j:j + 1], ALU.subtract, ALU.mult).then_inc(done, 1)

            def max_split(b, g):
                wait(dve, m_mm, 4, b, g + 1)
                if g:
                    wait(dve, m_in[g - 1], 48, b, 48)
                else:
                    wait(dve, m_in[3], 48, b - 1, 48)
                src = front_bank[0:16, 0:P]
                dve.tensor_scalar(m_parts[:, 0, :], src, -1.0, None, ALU.mult).then_inc(m_step, 1)
                wait(dve, m_step, 16, b, 4 * g + 1)
                dve.scalar_tensor_tensor(out=m_rest[:], in0=src, scalar=-1.0, in1=m_parts[:, 0, :],
                                         op0=ALU.mult, op1=ALU.subtract).then_inc(m_step, 1)
                wait(dve, m_step, 16, b, 4 * g + 2)
                dve.tensor_copy(m_parts[:, 1, :], m_rest[:]).then_inc(m_step, 1)
                wait(dve, m_step, 16, b, 4 * g + 3)
                dve.tensor_tensor(m_parts[:, 2, :], m_rest[:], m_parts[:, 1, :], ALU.subtract).then_inc(m_step, 1)

            def y_reciprocal(b, c, i):
                if i == 0:
                    for g in (2 * c, 2 * c + 1):
                        wait(dve, y_in[g], 32, b, 32)
                v = denom[:, P * i:P * i + P]
                dve.reciprocal(v, v).then_inc(y_rec, 1)

            def y_normalise(b, c):
                wait(dve, y_rec, 8, b, 4 * c + 4)
                dve.tensor_tensor(yT[:, c, :], yT[:, c, :], denom[:], ALU.mult).then_inc(y_nrm, 1)

            def iteration(t, par):
                for slot in range(SLOTS):
                    max_unit(t, par, slot)
                    b = t + 1
                    if slot - 1 in XT_SLOT and present(b):
                        n = XT_SLOT[slot - 1]
                        wait(dve, xt_hi, 2, b, n + 1)
                        wait(dve, v_mm, 2, b - 1, 2)
                        dve.tensor_tensor(xT_lo[:, n, :], front_bank[:], xT_hi[:, n, :],
                                          ALU.subtract).then_inc(xt_lo, 1)
                    if slot - 1 in QK_SLOT and present(b):
                        n = QK_SLOT[slot - 1]
                        wait(dve, qk_hi, 4, b, n + 1)
                        wait(dve, qk_lo, 4, b, n) if n else wait(dve, qk_lo, 4, b - 1, 4)
                        dve.tensor_tensor(qk_rest[:], front_bank[:], parts[:, n % 2, 0, :],
                                          ALU.subtract).then_inc(qk_r, 1)
                        wait(dve, qk_r, 4, b, n + 1)
                        dve.tensor_copy(parts[:, n % 2, 1, :], qk_rest[:]).then_inc(qk_mid, 1)
                    if slot - 1 in V_SLOT and present(b):
                        n = V_SLOT[slot - 1]
                        wait(dve, v_mm, 2, b, n + 1)
                        wait(dve, pv_mm, 12, b - 2, 12)
                        dst = v_aug[:, 1 - par, 2 * n:2 * n + 2, :, :].rearrange("p k h (d o) -> p k h d o", o=2)
                        dve.tensor_copy(dst[:, :, :, :, 0], front_bank[:].rearrange(
                            "p (k h d) -> p k h d", k=2, h=H)).then_inc(v_ev, 1)
                    if slot - 1 in MAX_SLOT:
                        g = MAX_SLOT[slot - 1]
                        mb = t if g < 4 else t + 1
                        if present(mb):
                            max_split(mb, g % 4)
                    b = t - 1
                    if slot in (7, 8, 9, 10) and present(b):
                        y_reciprocal(b, 1, slot - 7)
                    if slot == 11 and present(b):
                        y_normalise(b, 1)
                    if slot in (28, 29, 30, 31) and present(t):
                        y_reciprocal(t, 0, slot - 28)
                    if slot == 32 and present(t):
                        y_normalise(t, 0)
                    if slot - 1 in PROJ_SLOT and present(b):
                        n = PROJ_SLOT[slot - 1]
                        wait(dve, pr_mm, 2, b, n + 1)
                        wait(dve, res_in, 16, b, 16)
                        r = res[:, 1 - par, 2 * n:2 * n + 2, :]
                        dve.tensor_tensor(r, acc_bank[:].rearrange("p (j c) -> p j c", c=C), r,
                                          ALU.add).then_inc(res_add, 1)
                        wait(dve, res_add, 2, b, n + 1)
                        wait(dve, xt_mm, 2, b + 2, 2)
                        norm_tiles(res[:, 1 - par], 1, (2 * n, 2 * n + 1), b, 4 * n, ln2_done)
                    if slot - 1 in X2T_SLOT and present(b):
                        n = X2T_SLOT[slot - 1]
                        wait(dve, x2t_hi, 2, b, n + 1)
                        wait(dve, f1_mm, 8, b - 1, 4 * n + 4)
                        cols = slice(256 * n, 256 * n + 256)
                        dve.tensor_tensor(x2T_lo[:, :, cols], ffn_bank[:].rearrange("p (c q) -> p c q", c=CC),
                                          x2T_hi[:, :, cols], ALU.subtract).then_inc(x2t_lo, 1)
                    if slot in (31, 39) and present(b):
                        n = (31, 39).index(slot)
                        wait(dve, f2_mm, 8, b, 4 * n + 4)
                        wait(dve, b2_add, 4, b, 2 * n + 2)
                        r = res[:, 1 - par, 2 * n:2 * n + 2, :]
                        dve.tensor_tensor(r, acc_bank[:].rearrange("p (j c) -> p j c", c=C), r,
                                          ALU.add).then_inc(out_add, 1)
                    if slot == 34 and present(t + 2):
                        layer_norm_1(t + 2, par)

            def layer_norm_1(b, par):
                wait(dve, emb_in, 64, b, 64)
                wait(dve, x2t_mm, 2, b - 3, 2)
                norm_tiles(emb[:, par], 0, range(NT), b, 0, ln1_done)

            dve.wait_ge(const_ok, 7)
            layer_norm_1(0, 0)
            schedule(dve, iteration)

        @block.tensor
        def _(pe):
            pe.wait_ge(const_ok, 7)
            pe.wait_ge(w_step, 2)
            pe.matmul(acc_bank[:, 0:2], ones, w_sum[:], start=True, stop=True).then_inc(w_mm, 1)
            pe.wait_ge(w_step, W_QUANT_STEPS)
            evac = W_QUANT_STEPS
            w1q = raw_w1.rearrange("p (j c) -> p j c", c=C)
            w2q = raw_w2.rearrange("p (j c) -> p j c", c=FF)

            def four(pairs):
                for k, src in enumerate(pairs):
                    ins = pe.transpose(front_bank[:, P * k:P * k + P], src, ident[:])
                ins.then_inc(w_mm, 1)

            for k in range(FC // 2):
                if k:
                    evac += 1
                    pe.wait_ge(w_step, evac)
                four([w1q[:, 2 * k + i, P * c:P * c + P] for c in range(CC) for i in range(2)])
            for k in range(FC // 2):
                evac += 1
                pe.wait_ge(w_step, evac)
                four([w2q[:, c, P * (2 * k + i):P * (2 * k + i) + P] for i in range(2) for c in range(CC)])
            evac += 1
            for k in range(3):
                pe.wait_ge(w_step, evac)
                four([raw_attn[:, 2 * k + i, P * c:P * c + P] for c in range(CC) for i in range(2)])
                evac += 2 if k == 2 else 8
            pe.wait_ge(w_step, evac)
            four([raw_proj[:, i, P * c:P * c + P] for c in range(CC) for i in range(2)])
            pe.wait_ge(w_ready, 1)
            pe.wait_ge(aug_const_in, 128)

            def front_bank_free(t, slot):
                at = [s for s, _, _ in FRONT_USES].index(slot)
                back = 0
                while True:
                    at -= 1
                    if at < 0:
                        at, back = len(FRONT_USES) - 1, back + 1
                    if back > 1:
                        return
                    _, kind, n = FRONT_USES[at]
                    b = front_batch(kind, n, t - back)
                    if present(b):
                        break
                if kind == "xt":
                    wait(pe, xt_lo, 2, b, n + 1)
                elif kind == "qk":
                    wait(pe, qk_r, 4, b, n + 1)
                elif kind == "v":
                    wait(pe, v_ev, 2, b, n + 1)
                else:
                    wait(pe, m_step, 16, b, 4 * (n % 4) + 2)

            def st_unit(b, par, n):
                g, m = n // UNITS, n % UNITS
                if m == 0:
                    wait(pe, m_in[g], 48, b, 48)
                if n >= 2:
                    wait(pe, exp_done, 40, b, n - 1)
                else:
                    wait(pe, exp_done, 40, b - 1, 39 + n)
                blocks = st_blocks(m)
                for i, (h, kb, col) in enumerate(blocks):
                    q0 = kb * P
                    for rows, a, z in ((K_DIAGONAL, q0, q0 + P), (K_SHIFTED, q0 + P, T)):
                        if a < z:
                            ins = pe.matmul(st_bank[n % 2][:, col + a - q0:col + z - q0],
                                            k_aug[0:rows, par, GH * g + h, q0:q0 + P],
                                            q_aug[0:rows, par, GH * g + h, a:z], start=True, stop=True)
                ins.then_inc(st_mm, 1)

            def s_unit(t, par, slot):
                b, n = score_unit(t, slot)
                if not present(b):
                    return
                bp = par if b is t else 1 - par
                g, m = n // UNITS, n % UNITS
                if m == 0 and g % 2 == 0:
                    wait(pe, aug_in[g], 48, b, 48)
                    wait(pe, aug_in[g + 1], 48, b, 48)
                if n >= 2:
                    wait(pe, s_max, 40, b, n - 1)
                else:
                    wait(pe, s_max, 40, b - 1, 39 + n)
                for i, (h, qb, col) in enumerate(s_blocks(m)):
                    w = (qb + 1) * P
                    ins = pe.matmul(s_bank[n % 2][:, col:col + w],
                                    q_aug[0:K_SCORES, bp, GH * g + h, qb * P:qb * P + P],
                                    k_aug[0:K_SCORES, bp, GH * g + h, 0:w], start=True, stop=True)
                ins.then_inc(s_mm, 1)

            def pv(b, par, g, part):
                wait(pe, zero_done, 40, b, UNITS * g + (4, 8, 10)[part])
                if part == 0:
                    if g == 0:
                        wait(pe, v_ev, 2, b, 2)
                        wait(pe, y_ev, 4, b - 1, 4)
                    else:
                        wait(pe, y_ev, 4, b, g)
                for kb in ((0,), (1, 3), (2,))[part]:
                    q0 = kb * P
                    for h in range(GH):
                        unit, col = P_AT[h, kb]
                        ins = pe.matmul(pv_bank[32 * h:32 * h + 32, q0:T], v_aug[:, par, kb, GH * g + h, :],
                                        prob[:, unit, col:col + T - q0], start=(kb == 0), stop=(kb == 2))
                ins.then_inc(pv_mm, 1)

            def x_transpose(b, c):
                if c == 0:
                    wait(pe, ln1_done, 4, b, 4)
                for j in range(NT):
                    ins = pe.transpose(front_bank[:, P * j:P * j + P], xn[:, j, P * c:P * c + P], ident[:])
                ins.then_inc(xt_mm, 1)

            def qk_project(b, n):
                if n == 0:
                    wait(pe, xt_lo, 2, b, 2)
                terms = [(w, xx, c) for c in range(CC)
                         for w, xx in ((wqk_hi, xT_hi), (wqk_hi, xT_lo), (wqk_lo, xT_hi))]
                for i, (w, xx, c) in enumerate(terms):
                    ins = pe.matmul(front_bank[:], w[:, c, n, :], xx[:, c, :], start=(i == 0),
                                    stop=(i == len(terms) - 1))
                ins.then_inc(qk_mm, 1)

            def v_project(b, n):
                terms = [(w, xx, c) for c in range(CC)
                         for w, xx in ((wv_hi, xT_hi), (wv_hi, xT_lo), (wv_lo, xT_hi))]
                for j in range(2):
                    tok = slice(P * (2 * n + j), P * (2 * n + j) + P)
                    for i, (w, xx, c) in enumerate(terms):
                        ins = pe.matmul(front_bank[:, C * j:C * j + C], xx[:, c, tok], w[:, c, :], start=(i == 0),
                                        stop=(i == len(terms) - 1))
                ins.then_inc(v_mm, 1)

            def out_project(b, n):
                if n == 0:
                    wait(pe, y_nrm, 2, b, 2)
                    wait(pe, out_add, 2, b - 1, 2)
                else:
                    wait(pe, res_add, 2, b, 1)
                for j in range(2):
                    tok = slice(P * (2 * n + j), P * (2 * n + j) + P)
                    for c in range(CC):
                        ins = pe.matmul(acc_bank[:, C * j:C * j + C], yT[:, c, tok], wp[:, c, :], start=(c == 0),
                                        stop=(c == CC - 1))
                ins.then_inc(pr_mm, 1)

            def x2_transpose(b, n):
                wait(pe, ln2_done, 4, b, 2 * n + 2)
                if n == 0:
                    wait(pe, f1_relu, 16, b - 1, 16)
                else:
                    wait(pe, f1_relu, 16, b, 2)
                for c in range(CC):
                    for j in range(2):
                        at = 256 * c + P * j
                        ins = pe.transpose(ffn_bank[:, at:at + P], xn[:, 2 * n + j, P * c:P * c + P], ident[:])
                ins.then_inc(x2t_mm, 1)

            def ffn_in(b, n):
                half, u = n // 4, n % 4
                wait(pe, x2t_lo, 2, b, 1 if n == 0 else 2)
                if n >= 2:
                    wait(pe, f1_relu, 16, b, 2 * n)
                for i in range(2):
                    f = 2 * u + i
                    terms = [(xx, c) for c in range(CC) for xx in (x2T_hi, x2T_lo)]
                    for k, (xx, c) in enumerate(terms):
                        ins = pe.matmul(ffn_bank[:, 256 * i:256 * i + 256], w1T[:, c, P * f:P * f + P],
                                        xx[:, c, 256 * half:256 * half + 256], start=(k == 0),
                                        stop=(k == len(terms) - 1))
                ins.then_inc(f1_mm, 1)

            def ffn_out(b, n):
                half, u = n // 4, n % 4
                wait(pe, f1_lo, 8, b, n + 1)
                if n == 0:
                    wait(pe, res_add, 2, b, 2)
                elif n == 4:
                    wait(pe, out_add, 2, b, 1)
                for i in range(2):
                    f = 2 * u + i
                    for hh in (h_hi, h_lo):
                        for j in range(2):
                            first = u == 0 and i == 0 and hh is h_hi and j == 0
                            last = u == 3 and i == 1 and hh is h_lo
                            ins = pe.matmul(acc_bank[:, C * j:C * j + C], hh[:, f, P * j:P * j + P], w2T[:, f, :],
                                            start=first, stop=last, skip_group_check=True)
                ins.then_inc(f2_mm, 1)

            def iteration(t, par):
                for slot in range(SLOTS):
                    if present(t):
                        st_unit(t, par, slot)
                    s_unit(t, par, slot)
                    if slot % 10 in PV_SLOT:
                        part = PV_SLOT[slot % 10]
                        g = slot // 10 - (part > 0)
                        b, bp = (t, par) if g >= 0 else (t - 1, 1 - par)
                        if present(b):
                            pv(b, bp, g % 4, part)
                    b = t + 1
                    front = slot in XT_SLOT or slot in QK_SLOT or slot in V_SLOT
                    if front and present(b):
                        front_bank_free(t, slot)
                        if slot in XT_SLOT:
                            x_transpose(b, XT_SLOT[slot])
                        elif slot in QK_SLOT:
                            qk_project(b, QK_SLOT[slot])
                        else:
                            v_project(b, V_SLOT[slot])
                    if slot in MAX_SLOT:
                        g = MAX_SLOT[slot]
                        mb = t if g < 4 else t + 1
                        if present(mb):
                            front_bank_free(t, slot)
                            g %= 4
                            wait(pe, s_max, 40, mb, UNITS * g + UNITS)
                            pe.transpose(front_bank[0:16, 0:P], row_max[:, g % 2, :], ident[:]).then_inc(m_mm, 1)
                    b = t - 1
                    if present(b):
                        if slot in PROJ_SLOT:
                            out_project(b, PROJ_SLOT[slot])
                        if slot in X2T_SLOT:
                            x2_transpose(b, X2T_SLOT[slot])
                        if slot in F1_SLOT:
                            ffn_in(b, F1_SLOT[slot])
                        if slot in F2_SLOT:
                            ffn_out(b, F2_SLOT[slot])

            schedule(pe, iteration)


W_QUANT_STEPS = 9


def constants():
    bf = np.dtype("bfloat16")
    start = 2.0 ** (-8.0 / H)
    slopes = np.array([start ** (i + 1) for i in range(H)], np.float32)
    cut, rest = [], slopes.copy()
    for _ in range(3):
        p = rest.astype(bf)
        cut.append(p)
        rest = (rest - p.astype(np.float32)).astype(np.float32)
    pos = (np.arange(T) - T // 2).astype(bf)
    q = np.zeros((ALIBI_ROWS + SUB_ROWS, H, T), bf)
    k = np.zeros((ALIBI_ROWS + 3 + SUB_ROWS, H, T), bf)
    for i in range(3):
        q[i] = pos[None, :]
        k[i] = -cut[i][:, None]
        q[3 + i] = cut[i][:, None]
        k[3 + i] = pos[None, :]
    k[ALIBI_ROWS:ALIBI_ROWS + 3] = 1.0
    within = np.arange(T) % P
    for j in range(SUB_ROWS):
        q[ALIBI_ROWS + j] = np.where(within < SUB * (j + 1), MASKED, 0.0)[None, :]
        k[ALIBI_ROWS + 3 + j] = (within // SUB == j + 1)[None, :]
    return q.reshape(-1, H * T), k.reshape(-1, H * T)


def kernel(x, L0_tok_weight, L0_attn_W_attn, L0_attn_W_proj, L0_ffn_W1, L0_ffn_b1, L0_ffn_W2, L0_ffn_b2):
    import concourse.bacc as bacc
    from concourse.bass_utils import run_bass_kernel_spmd

    q_const, k_const = constants()
    given = {
        "x": x, "table": L0_tok_weight, "w_attn": L0_attn_W_attn, "w_proj": L0_attn_W_proj, "w1": L0_ffn_W1,
        "b1": L0_ffn_b1, "w2": L0_ffn_W2, "b2": L0_ffn_b2, "q_const": q_const, "k_const": k_const,
    }
    nc = bacc.Bacc("TRN2", target_bir_lowering=False, num_devices=1)
    arrays, args = {}, []
    for name, a in given.items():
        a = np.ascontiguousarray(a)
        arrays[name] = a
        args.append(nc.dram_tensor(name, a.shape, mybir.dt.from_np(a.dtype), kind="ExternalInput").ap())
    out = nc.dram_tensor("out", [NB * T, C], F32, kind="ExternalOutput").ap()
    block_program(nc, *args, out)
    r = run_bass_kernel_spmd(nc, [arrays], core_ids=[0])
    return r.results[0]["out"].reshape(NB, T, C)
```

```python
from contextlib import ExitStack

import numpy as np

import concourse.bass as bass
from concourse import mybir

F32 = mybir.dt.float32
F32R = mybir.dt.float32r
BF16 = mybir.dt.bfloat16
I32 = mybir.dt.int32
ACT = mybir.ActivationFunctionType
ALU = mybir.AluOpType
AX = mybir.AxisListType

P = 128
NB, T, C, FF = 32, 512, 256, 1024
H, D = 16, 16
NT = T // P
CC = C // P
FC = FF // P
GROUPS, GH = 4, 4
UNITS = 10
SLOTS = GROUPS * UNITS
LEAD = 17
EPS = 1e-5
MASKED = -1.0e38
ALIBI_ROWS = 6
PART_ROWS = 6 * D
MAX_ROW = ALIBI_ROWS + PART_ROWS
K_SCORES = MAX_ROW
K_SHIFTED = MAX_ROW + 3
SUB = 16
SUB_ROWS = P // SUB - 1
K_DIAGONAL = K_SHIFTED + SUB_ROWS
Q_SPREAD = [(0, 3, 0, 0), (3, 2, 1, 1), (5, 1, 1, 1)]
K_SPREAD = [(0, 3, 0, 1), (3, 2, 0, 0), (5, 1, 1, 1)]


ATTN_CHUNKS = 4
_attn = [4 * CC, 8 * CC, 8 * CC + 2, 8 * CC + 3]
W_SUMMED = _attn[-1] + 2
W_TERNARY = [W_SUMMED + 3 + 4, W_SUMMED + 3 + 8]
W_EVACUATED = _attn + [W_TERNARY[1] + 1 + k for k in range(FC)]


class Batch:

    def __init__(self, reg, off=0):
        self.reg, self.off = reg, off

    def __add__(self, n):
        return Batch(self.reg, self.off + n)

    def __sub__(self, n):
        return Batch(self.reg, self.off - n)

    def times(self, n, more=0):
        return self.reg * n + (self.off * n + more)


def present(b):
    return isinstance(b, Batch) or 0 <= b < NB


def upto(b, per, n):
    return b.times(per, n) if isinstance(b, Batch) else b * per + n


def wait(eng, sem, per, b, n):
    if present(b) and (isinstance(b, Batch) or b * per + n > 0):
        eng.wait_ge(sem, upto(b, per, n))


def row(b, scale=1):
    return b.times(scale) if isinstance(b, Batch) else b * scale


def s_blocks(n):
    if n < 4:
        return [(n, 3, 0)]
    if n < 8:
        return [(n - 4, 2, 0), (n - 4, 0, 384)]
    return [(2 * (n - 8), 1, 0), (2 * (n - 8) + 1, 1, 256)]


def st_blocks(n):
    if n < 4:
        return [(n, 0, 0)]
    if n < 8:
        return [(n - 4, 1, 0), (n - 4, 3, 384)]
    return [(2 * (n - 8), 2, 0), (2 * (n - 8) + 1, 2, 256)]


P_AT = {(h, kb): (n, col) for n in range(UNITS) for h, kb, col in st_blocks(n)}

XT_SLOT = {0: 0, 2: 1}
V_SLOT = {4: 0, 6: 1}
QK_SLOT = {9: 0, 13: 1, 18: 2, 21: 3}
MAX_SLOT = {5: 1, 15: 2, 25: 3, 34: 4}
PV_SLOT = {6: 0, 0: 1, 2: 2}
PROJ_SLOT = {13: 0, 14: 1}
X2T_SLOT = {18: 0, 19: 1}
F1_SLOT = {20: 0, 23: 1, 25: 2, 28: 3, 29: 4, 33: 5, 35: 6, 37: 7}
F2_SLOT = {23: 0, 26: 1, 28: 2, 31: 3, 35: 4, 38: 5, 39: 6, 3: 7}
Y_OUT_AT = 2
INV_SLOT = {27: 0, 6: 1}
INV_OUT_SLOT = {28: 0, 7: 1}
NORM_SLOT = {33: 0, 11: 1}
SPREAD_SLOT = {13: 0, 15: 1, 22: 2, 23: 3}
SPREAD_LAG = 4
STAT2_LAG, NORM2_LAG = 1, 3
B2_SLOT = {20: 0, 23: 1}
OUT_ADD_SLOT = {32: 0, 3: 1}
STORE_SLOT = 5
RESIDUAL_SLOT = 10
GATHER_SLOT = {14: 0, 16: 1, 18: 2, 19: 3}
LN1_STAT_SLOT = {29: 0, 30: 1}
LN1_SLOT = {33: (0, 1), 36: (2, 3)}

OUT_BANK_GROUPS = (1, 2)
FRONT_USES = sorted([(s, "xt", n) for s, n in XT_SLOT.items()] + [(s, "qk", n) for s, n in QK_SLOT.items()]
                    + [(s, "v", n) for s, n in V_SLOT.items()]
                    + [(s, "max", n) for s, n in MAX_SLOT.items() if n not in OUT_BANK_GROUPS])


def slot_of(slots, n):
    return [s for s, m in slots.items() if m == n][0]


assert slot_of(OUT_ADD_SLOT, 1) <= slot_of(MAX_SLOT, 1) < slot_of(PROJ_SLOT, 0)
assert slot_of(PROJ_SLOT, 0) < slot_of(MAX_SLOT, 2) < slot_of(X2T_SLOT, 1)


def front_batch(kind, n, t):
    return t if kind == "max" and n < 4 else t + 1


def block_program(nc, x, table, w_attn, w_proj, w1, b1, w2, b2, q_const, k_const, out):
    with ExitStack() as ctx:
        def sb(name, shape, dt):
            return ctx.enter_context(nc.sbuf_tensor(name, shape, dt))

        def bank(name):
            return ctx.enter_context(nc.psum_tensor(name, [P, 512], F32))

        def sem(name):
            return ctx.enter_context(nc.semaphore(name))

        ids = sb("ids", [P, NT], I32)
        emb = sb("emb", [P, 2, NT, C], F32)
        res = sb("res", [P, 2, NT, C], F32)
        xn = sb("xn", [P, NT, C], F32)
        xT_hi = sb("xT_hi", [P, CC, T], F32R)
        xT_lo = sb("xT_lo", [P, CC, T], F32R)
        x2T_hi = sb("x2T_hi", [P, CC, T], F32R)
        x2T_lo = sb("x2T_lo", [P, CC, T], F32R)
        parts = sb("parts", [P, 2, 3, T], BF16)
        qk_rest = sb("qk_rest", [P, T], F32)
        q_aug = sb("q_aug", [P, 2, H, T], BF16)
        k_aug = sb("k_aug", [P, 2, H, T], BF16)
        v_aug = sb("v_aug", [P, 2, NT, H, 2 * D], F32)
        prob = sb("prob", [P, UNITS, T], F32)
        y_raw = sb("y_raw", [P, T], F32)
        yT = sb("yT", [P, CC, T], F32)
        denom = sb("denom", [4 * 16, P], F32)
        inv_denom = sb("inv_denom", [P, T], F32)
        h_full = sb("h_full", [P, 2, 2, 256], F32)
        h_hi = sb("h_hi", [P, FC, 256], F32R)
        h_lo = sb("h_lo", [P, FC, 256], F32R)
        wqk_hi = sb("wqk_hi", [P, CC, 4, P], F32R)
        wqk_lo = sb("wqk_lo", [P, CC, 4, P], F32R)
        wv_hi = sb("wv_hi", [P, CC, C], F32R)
        wv_lo = sb("wv_lo", [P, CC, C], F32R)
        wp = sb("wp", [P, CC, C], F32)
        w1T = sb("w1T", [P, CC, FF], F32R)
        w2T = sb("w2T", [P, FC, C], F32R)
        b1_col = sb("b1_col", [P, FC], F32)
        b2_row = sb("b2_row", [P, C], F32)
        ident = sb("ident", [P, P], F32)
        mask = sb("mask", [P, T], BF16)
        row_max = sb("row_max", [P, 2, 16], F32)
        m_parts = sb("m_parts", [16, 3, P], BF16)
        m_rest = sb("m_rest", [16, P], F32)
        stats = sb("stats", [P, 2, NT, 6], F32)
        mean_var = sb("mean_var", [P, 2, NT, 2], F32)
        rstd = sb("rstd", [P, 2, NT], F32)
        neg_half = sb("neg_half", [P, NT], F32)
        w_sum = sb("w_sum", [P, 2], F32)
        w_thr = sb("w_thr", [P, 4], F32)
        ones = qk_rest[:, 0:P]
        raw_attn = prob[:, 0:3, :].rearrange("p a b -> p (a b)").rearrange("p (j c) -> p j c", c=C)
        raw_proj = prob[:, 3, :].rearrange("p (j c) -> p j c", c=C)
        raw_w1 = prob[:, 4:8, :].rearrange("p a b -> p (a b)")
        raw_w2 = res[:].rearrange("p a b c -> p (a b c)")
        below = h_full[:].rearrange("p a b c -> p (a b c)")

        s_bank = [bank("s_bank0"), bank("s_bank1")]
        st_bank = [bank("st_bank0"), bank("st_bank1")]
        pv_bank = bank("pv_bank")
        front_bank = bank("front_bank")
        ffn_bank = bank("ffn_bank")
        acc_bank = bank("acc_bank")
        proj_bank = [acc_bank, ffn_bank]
        x2t_bank = [ffn_bank, acc_bank]

        def max_bank(g):
            return acc_bank if g in OUT_BANK_GROUPS else front_bank

        w_bank = [front_bank, ffn_bank, acc_bank, pv_bank]

        scratch = nc.dram_tensor("parts_scratch", [4, 3, P, T], BF16, kind="Internal").ap()
        inv_scratch = nc.dram_tensor("inv_scratch", [CC, 8, 1, T], F32, kind="Internal").ap()

        attn_in, ffn_w_in, bias_in = sem("attn_in"), sem("ffn_w_in"), sem("bias_in")
        const_ok = sem("const_ok")
        ident_ok = sem("ident_ok")
        aug_const_in = sem("aug_const_in")
        w_step = sem("w_step")
        w_mm = sem("w_mm")
        w_ready = sem("w_ready")
        ids_in = sem("ids_in")
        emb_in = sem("emb_in")
        res_in = sem("res_in")
        ln_step = [sem("ln1_step"), sem("ln2_step")]
        rstd_step = [sem("rstd1_step"), sem("rstd2_step")]
        ln1_done = sem("ln1_done")
        xt_mm, xt_hi, xt_lo = sem("xt_mm"), sem("xt_hi"), sem("xt_lo")
        qk_mm, qk_hi, qk_r = sem("qk_mm"), sem("qk_hi"), sem("qk_r")
        qk_mid, qk_lo = sem("qk_mid"), sem("qk_lo")
        scratch_w = [sem(f"scratch_w{n}") for n in range(4)]
        aug_in = [sem(f"aug_in{n}") for n in range(4)]
        v_mm, v_ev = sem("v_mm"), sem("v_ev")
        s_mm, s_max = sem("s_mm"), sem("s_max")
        m_mm, m_step = sem("m_mm"), sem("m_step")
        m_in = [sem(f"m_in{g}") for g in range(GROUPS)]
        st_mm, exp_done, zero_done = sem("st_mm"), sem("exp_done"), sem("zero_done")
        pv_mm, y_ev = sem("pv_mm"), sem("y_ev")
        y_in = [sem(f"y_in{g}") for g in range(GROUPS)]
        y_rec, y_nrm = sem("y_rec"), sem("y_nrm")
        inv_w = sem("inv_w")
        inv_in = [sem(f"inv_in{c}") for c in range(CC)]
        pr_mm, res_add = sem("pr_mm"), sem("res_add")
        ln2_done = sem("ln2_done")
        x2t_mm, x2t_hi, x2t_lo = sem("x2t_mm"), sem("x2t_hi"), sem("x2t_lo")
        f1_mm, f1_relu, f1_hi, f1_lo = sem("f1_mm"), sem("f1_relu"), sem("f1_hi"), sem("f1_lo")
        f2_mm, out_add = sem("f2_mm"), sem("out_add")
        b2_add = sem("b2_add")
        out_w = sem("out_w")

        block = ctx.enter_context(nc.Block())

        def wait_alone(eng, sem, per, b, n):
            wait(eng, sem, per, b, n)
            if isinstance(b, Batch):
                eng.nop(nofuse=True)

        def schedule(eng, iteration):
            for t in (-1, 0, 1):
                iteration(t, t % 2)
            with eng.Fori(2, NB - 3, 2) as t:
                iteration(Batch(t), 0)
                iteration(Batch(t, 1), 1)
            for t in (NB - 2, NB - 1, NB, NB + 1):
                iteration(t, t % 2)

        def score_unit(t, slot):
            u = slot + LEAD
            return (t, u) if u < SLOTS else (t + 1, u - SLOTS)

        @block.sync
        def _(sp):
            def load_ids(b):
                wait_alone(sp, emb_in, 64, b - 1, 64)
                with nc.allow_non_contiguous_dma(reason="2 KB of ids"):
                    src = x[bass.ds(row(b), 1), :].rearrange("o (j p) -> p (o j)", p=P)
                    sp.dma_start(ids[:], src).then_inc(ids_in, 16)

            def parts_out(b, n):
                wait_alone(sp, qk_lo, 4, b, n + 1)
                wait_alone(sp, aug_in[n], 48, b - 1, 48)
                sp.dma_start(scratch[n].rearrange("a p t -> p a t"), parts[:, n % 2, :, :]).then_inc(scratch_w[n], 16)

            def spread(b, par, n):
                aug, plan = (q_aug, Q_SPREAD) if n % 2 == 0 else (k_aug, K_SPREAD)
                h0 = 8 * (n // 2)
                wait_alone(sp, scratch_w[n], 16, b, 16)
                wait_alone(sp, st_mm, 40, b - 2, 40)
                for g0, count, part, step in plan:
                    for_part = scratch[n, part:part + (count if step else 1)]
                    src = for_part.rearrange("a (d h) t -> a d (h t)", h=8)
                    if not step and count > 1:
                        src = src.to_broadcast([count, D, 8 * T])
                    r0 = ALIBI_ROWS + g0 * D
                    dst = aug[r0:r0 + count * D, par, h0:h0 + 8, :].rearrange("p h t -> p (h t)")
                    sp.dma_start(dst, src).then_inc(aug_in[n], 16)

            def iteration(t, par):
                for slot in range(SLOTS):
                    if slot == STORE_SLOT and present(t - 2):
                        wait_alone(sp, out_add, 2, t - 2, 2)
                        dst = out[bass.ds(row(t - 2, T), T), :].rearrange("(j p) c -> p j c", p=P)
                        sp.dma_start(dst, res[:, par]).then_inc(out_w, 16)
                    if slot == RESIDUAL_SLOT and present(t):
                        wait_alone(sp, out_w, 16, t - 2, 16)
                        wait_alone(sp, emb_in, 64, t, 64)
                        if not isinstance(t, Batch) and t < 2:
                            sp.wait_ge(w_ready, 1)
                        sp.dma_start(res[:, par], emb[:, par]).then_inc(res_in, 16)
                    if slot == 0 and present(t) and present(t + 2):
                        load_ids(t + 2)
                    if slot in SPREAD_SLOT and present(t + 1):
                        parts_out(t + 1, SPREAD_SLOT[slot])
                    if slot - 2 in MAX_SLOT:
                        g = MAX_SLOT[slot - 2]
                        b, bp = (t, par) if g < 4 else (t + 1, 1 - par)
                        g %= 4
                        if present(b):
                            wait_alone(sp, m_step, 16, b, 4 * g + 4)
                            wait_alone(sp, st_mm, 40, b - 2, 40)
                            for k in range(3):
                                dst = q_aug[MAX_ROW + k:MAX_ROW + k + 1, bp, GH * g:GH * g + GH, :]
                                sp.dma_start(dst.rearrange("p h t -> p (h t)"),
                                             m_parts[:, k, :]).then_inc(m_in[g], 16)
                    if slot - SPREAD_LAG in SPREAD_SLOT and present(t + 1):
                        spread(t + 1, 1 - par, SPREAD_SLOT[slot - SPREAD_LAG])
                    if slot % 10 == Y_OUT_AT:
                        g = slot // 10 - 1
                        b = t if g >= 0 else t - 1
                        g %= 4
                        if present(b):
                            wait_alone(sp, y_ev, 4, b, g + 1)
                            wait_alone(sp, pr_mm, 2, b - 1, 2)
                            wait_alone(sp, inv_w, 32, b - 1, 16 + 16 * (g // 2))
                            rows = slice(64 * (g % 2), 64 * (g % 2) + 64)
                            sp.dma_start(yT[rows, g // 2, :], y_raw[0:127:2, :]).then_inc(y_in[g], 16)
                            sp.dma_start(denom[16 * g:16 * g + 16, :], y_raw[1:128:32, :]).then_inc(y_in[g], 16)
                    if slot in INV_OUT_SLOT:
                        c = INV_OUT_SLOT[slot]
                        b = t - c
                        if present(b):
                            wait_alone(sp, y_rec, 2, b, c + 1)
                            wait_alone(sp, inv_in[c], 16, b - 1, 16)
                            sp.dma_start(inv_scratch[c].rearrange("h o (a n) -> (h o a) n", a=4),
                                         denom[32 * c:32 * c + 32, :]).then_inc(inv_w, 16)
                    if slot - 2 in INV_OUT_SLOT:
                        c = INV_OUT_SLOT[slot - 2]
                        b = t - c
                        if present(b):
                            wait_alone(sp, inv_w, 32, b, 16 * c + 16)
                            wait_alone(sp, y_nrm, 2, b if c else b - 1, 1 if c else 2)
                            sp.dma_start(inv_denom[:], inv_scratch[c].to_broadcast([8, D, T])).then_inc(inv_in[c], 16)

            load_ids(0)
            with nc.allow_non_contiguous_dma(reason="small columns"):
                sp.dma_start(raw_attn, w_attn.rearrange("(j p) c -> p j c", p=P)).then_inc(attn_in, 16)
                sp.dma_start(raw_proj, w_proj.rearrange("(j p) c -> p j c", p=P)).then_inc(attn_in, 16)
                sp.dma_start(raw_w1.rearrange("p (j c) -> p j c", c=C),
                             w1.rearrange("(j p) c -> p j c", p=P)).then_inc(ffn_w_in, 16)
                sp.dma_start(raw_w2.rearrange("p (j c) -> p j c", c=FF),
                             w2.rearrange("(j p) c -> p j c", p=P)).then_inc(ffn_w_in, 16)
                sp.dma_start(b1_col[:], b1.rearrange("(j p) -> p j", p=P)).then_inc(bias_in, 16)
                sp.dma_start(b2_row[:], b2.rearrange("(a c) -> a c", a=1).to_broadcast([P, C])).then_inc(bias_in, 16)
            for par in range(2):
                sp.dma_start(q_aug[0:ALIBI_ROWS, par, :, :].rearrange("p h t -> p (h t)"),
                             q_const[0:ALIBI_ROWS, :]).then_inc(aug_const_in, 16)
                sp.dma_start(k_aug[0:ALIBI_ROWS, par, :, :].rearrange("p h t -> p (h t)"),
                             k_const[0:ALIBI_ROWS, :]).then_inc(aug_const_in, 16)
                sp.dma_start(q_aug[K_SHIFTED:K_DIAGONAL, par, :, :].rearrange("p h t -> p (h t)"),
                             q_const[ALIBI_ROWS:, :]).then_inc(aug_const_in, 16)
                sp.dma_start(k_aug[MAX_ROW:K_DIAGONAL, par, :, :].rearrange("p h t -> p (h t)"),
                             k_const[ALIBI_ROWS:, :]).then_inc(aug_const_in, 16)
            load_ids(1)
            schedule(sp, iteration)
            sp.wait_ge(out_w, 16 * NB)

        @block.gpsimd
        def _(pool):
            pool.memset(ident[:], 0.0).then_inc(const_ok, 1)
            pool.memset(ones, 1.0).then_inc(const_ok, 1)
            pool.memset(mask[:], 0.0).then_inc(const_ok, 1)
            pool.memset(neg_half[:], -0.5).then_inc(const_ok, 1)
            pool.wait_ge(const_ok, 4)
            pool.affine_select(out=ident[:], in_=ident[:], compare_op=ALU.not_equal, fill=1.0, base=0,
                               pattern=[[-1, P]], channel_multiplier=1).then_inc(ident_ok, 1)
            pool.affine_select(out=mask[:, T - P:T], in_=mask[:, T - P:T], compare_op=ALU.is_ge, fill=MASKED,
                               base=0, pattern=[[-1, P]], channel_multiplier=1).then_inc(const_ok, 1)
            pool.memset(v_aug[:].rearrange("p a b c d -> p (a b c d)"), 1.0).then_inc(const_ok, 1)

            def gather(b, par, tiles):
                if tiles[0] == 0:
                    pool.wait_ge(ids_in, upto(b, 16, 16))
                    wait(pool, res_in, 16, b - 2, 16)
                    wait_alone(pool, ln1_done, 4, b - 2, 4)
                for j in tiles:
                    pool.indirect_dma_start(
                        out=emb[:, par, j, :], out_offset=None, in_=table,
                        in_offset=bass.IndirectOffsetOnAxis(ap=ids[:, j:j + 1], axis=0)).then_inc(emb_in, 16)

            def zero_future(b, n):
                wait_alone(pool, exp_done, 40, b, n + 1)
                m = n % UNITS
                if m < 4:
                    v, pat = prob[:, m, 0:P], [[1, P]]
                elif m < 8:
                    v, pat = prob[:, m, :].rearrange("p (a q) -> p a q", q=P)[:, 0:4:3, :], [[0, 2], [1, P]]
                else:
                    v, pat = prob[:, m, :].rearrange("p (a q) -> p a q", q=P)[:, 0:4:2, :], [[0, 2], [1, P]]
                pool.affine_select(out=v, in_=v, compare_op=ALU.is_ge, fill=0.0, base=0,
                                   pattern=pat, channel_multiplier=-1).then_inc(zero_done, 1)

            def qk_low(b, n):
                pool.wait_ge(qk_mid, upto(b, 4, n + 1))
                wait(pool, scratch_w[(n - 2) % 4], 16, b if n >= 2 else b - 1, 16)
                pool.tensor_tensor(parts[:, n % 2, 2, :], qk_rest[:], parts[:, n % 2, 1, :],
                                   ALU.subtract).then_inc(qk_lo, 1)

            def hidden_low(b, n):
                pool.wait_ge(f1_hi, upto(b, 8, n + 1))
                wait(pool, f2_mm, 8, b if n >= 4 else b - 1, (n - 4) % 8 + 1)
                u = n % 4
                pool.tensor_tensor(h_lo[:, 2 * u:2 * u + 2, :], h_full[:, n % 2], h_hi[:, 2 * u:2 * u + 2, :],
                                   ALU.subtract).then_inc(f1_lo, 1)

            def add_b2(b, par, j):
                pool.wait_ge(ln2_done, upto(b, 4, 2 * j + 2))
                for i in range(2):
                    pool.tensor_tensor(res[:, par, 2 * j + i, :], res[:, par, 2 * j + i, :], b2_row[:],
                                       ALU.add).then_inc(b2_add, 1)

            def y_normalise(b, c):
                pool.wait_ge(y_in[2 * c], upto(b, 32, 32))
                pool.wait_ge(inv_in[c], upto(b, 16, 16))
                pool.tensor_tensor(yT[:, c, :], yT[:, c, :], inv_denom[:], ALU.mult).then_inc(y_nrm, 1)

            def reciprocal_root(b, which, half):
                t0, t1 = (0, NT) if which == 0 else (2 * half, 2 * half + 2)
                wait_alone(pool, ln_step[which], 2 * NT, b, 2 * NT if which == 0 else 4 * half + 4)
                pool.tensor_scalar(rstd[:, which, t0:t1], mean_var[:, which, t0:t1, 1], EPS, None,
                                   ALU.add).then_inc(rstd_step[which], 1)
                pool.wait_ge(rstd_step[which], upto(b, 2 + 2 * which, 2 * half + 1))
                pool.tensor_tensor(rstd[:, which, t0:t1], rstd[:, which, t0:t1], neg_half[:, t0:t1],
                                   ALU.pow).then_inc(rstd_step[which], 1)

            def iteration(t, par):
                for slot in range(SLOTS):
                    if slot in NORM_SLOT:
                        c = NORM_SLOT[slot]
                        if present(t - c):
                            y_normalise(t - c, c)
                    if present(t):
                        zero_future(t, slot)
                    if slot in GATHER_SLOT and present(t) and present(t + 2):
                        gather(t + 2, par, (GATHER_SLOT[slot],))
                    if slot - STAT2_LAG in PROJ_SLOT and present(t - 1):
                        reciprocal_root(t - 1, 1, PROJ_SLOT[slot - STAT2_LAG])
                    if slot == max(LN1_STAT_SLOT) + 1 and present(t + 2):
                        reciprocal_root(t + 2, 0, 0)
                    if slot - 1 in QK_SLOT and present(t + 1):
                        qk_low(t + 1, QK_SLOT[slot - 1])
                    if slot in B2_SLOT and present(t - 1):
                        add_b2(t - 1, 1 - par, B2_SLOT[slot])
                    if slot in F1_SLOT and present(t - 1):
                        hidden_low(t - 1, F1_SLOT[slot])

            gather(0, 0, range(NT))
            reciprocal_root(0, 0, 0)
            gather(1, 1, range(NT))
            pool.wait_ge(bias_in, 32)
            schedule(pool, iteration)

        @block.scalar
        def _(act):
            def split_high(dst, src, mm, done, per, b, n):
                wait(act, mm, per, b, n + 1)
                act.copy(dst, src).then_inc(done, 1)

            def exp_unit(b, n):
                g, m = n // UNITS, n % UNITS
                act.wait_ge(st_mm, upto(b, 40, n + 1))
                part = 1 if m < 4 else 2 if m < 8 else 3
                if m in (0, 4, 8):
                    if g:
                        act.wait_ge(pv_mm, upto(b, 12, 3 * (g - 1) + part))
                    else:
                        wait(act, pv_mm, 12, b - 1, 9 + part)
                act.activation(prob[:, m, :], st_bank[n % 2][:], ACT.Exp).then_inc(exp_done, 1)

            def iteration(t, par):
                for slot in range(SLOTS):
                    if present(t):
                        exp_unit(t, slot)
                    b = t + 1
                    if slot in XT_SLOT and present(b):
                        n = XT_SLOT[slot]
                        wait(act, qk_mm, 4, b - 1, 4)
                        split_high(xT_hi[:, n, :], front_bank[:], xt_mm, xt_hi, 2, b, n)
                    if slot in QK_SLOT and present(b):
                        n = QK_SLOT[slot]
                        wait(act, scratch_w[(n - 2) % 4], 16, b if n >= 2 else b - 1, 16)
                        split_high(parts[:, n % 2, 0, :], front_bank[:], qk_mm, qk_hi, 4, b, n)
                    if slot - 1 in QK_SLOT and present(b):
                        n = QK_SLOT[slot - 1]
                        act.wait_ge(qk_r, upto(b, 4, n + 1))
                        act.copy(parts[:, n % 2, 1, :], qk_rest[:]).then_inc(qk_mid, 1)
                    if slot in V_SLOT and present(b):
                        n = V_SLOT[slot]
                        act.wait_ge(v_mm, upto(b, 2, n + 1))
                        wait(act, pv_mm, 12, b - 2, 12)
                        dst = v_aug[:, 1 - par, 2 * n:2 * n + 2, :, :].rearrange("p k h (d o) -> p k h d o", o=2)
                        act.copy(dst[:, :, :, :, 0], front_bank[:].rearrange(
                            "p (k h d) -> p k h d", k=2, h=H)).then_inc(v_ev, 1)
                    if slot % 10 == Y_OUT_AT:
                        g = slot // 10 - 1
                        b = t if g >= 0 else t - 1
                        g %= 4
                        if present(b):
                            act.wait_ge(pv_mm, upto(b, 12, 3 * g + 3))
                            wait(act, y_in[(g - 1) % 4], 32, b if g else b - 1, 32)
                            act.copy(y_raw[:], pv_bank[:]).then_inc(y_ev, 1)
                    b = t - 1
                    if slot in X2T_SLOT and present(b):
                        n = X2T_SLOT[slot]
                        wait(act, f1_mm, 8, b - 1, 4 * n + 4)
                        split_high(x2T_hi[:, :, 256 * n:256 * n + 256],
                                   x2t_bank[n][:].rearrange("p (c q) -> p c q", c=CC), x2t_mm, x2t_hi, 2, b, n)
                    if slot in F1_SLOT and present(b):
                        n = F1_SLOT[slot]
                        u = n % 4
                        act.wait_ge(f1_mm, upto(b, 8, n + 1))
                        wait(act, f1_lo, 8, b if n >= 2 else b - 1, (n - 2) % 8 + 1)
                        for i in range(2):
                            act.activation(h_full[:, n % 2, i, :], ffn_bank[:, 256 * i:256 * i + 256], ACT.Relu,
                                           bias=b1_col[:, 2 * u + i:2 * u + i + 1]).then_inc(f1_relu, 1)
                        act.wait_ge(f1_relu, upto(b, 16, 2 * n + 2))
                        wait(act, f2_mm, 8, b if n >= 4 else b - 1, (n - 4) % 8 + 1)
                        act.copy(h_hi[:, 2 * u:2 * u + 2, :], h_full[:, n % 2]).then_inc(f1_hi, 1)

            act.wait_ge(bias_in, 32)
            act.wait_ge(w_ready, 1)
            schedule(act, iteration)

        @block.vector
        def _(dve):
            def max_unit(t, par, slot):
                b, n = score_unit(t, slot)
                if not present(b):
                    return
                g, m = n // UNITS, n % UNITS
                if m == 0:
                    wait(dve, m_mm, 4, b if g >= 2 else b - 1, (g - 2) % 4 + 1)
                wait_alone(dve, s_mm, 40, b, n + 1)
                blocks = s_blocks(m)
                for i, (h, qb, col) in enumerate(blocks):
                    w = (qb + 1) * P
                    bank_cols = s_bank[n % 2][:, col:col + w]
                    ins = dve.tensor_tensor_reduce(bank_cols, bank_cols, mask[:, T - w:T], 1.0, MASKED,
                                                   ALU.add, ALU.max, row_max[:, g % 2, GH * h + qb:GH * h + qb + 1])
                ins.then_inc(s_max, 1)

            def statistics(src, which, tiles, b, base):
                for j in tiles:
                    dve.bn_stats(stats[:, which, j, :], src[:, j, :]).then_inc(ln_step[which], 1)
                wait_alone(dve, ln_step[which], 2 * NT, b, base + len(tiles))
                for j in tiles:
                    dve.bn_aggr(mean_var[:, which, j, :], stats[:, which, j, :]).then_inc(ln_step[which], 1)

            def normalise(src, which, tiles, b, done):
                if tiles[0] == 0:
                    if which == 0:
                        wait(dve, x2t_mm, 2, b - 3, 2)
                    else:
                        wait(dve, xt_mm, 2, b + 2, 2)
                wait(dve, rstd_step[which], 2 + 2 * which, b, 2 if which == 0 else tiles[0] + 2)
                for j in tiles:
                    dve.tensor_scalar(xn[:, j, :], src[:, j, :], mean_var[:, which, j, 0:1],
                                      rstd[:, which, j:j + 1], ALU.subtract, ALU.mult).then_inc(done, 1)

            def max_split(b, g):
                dve.wait_ge(m_mm, upto(b, 4, g + 1))
                if g:
                    dve.wait_ge(m_in[g - 1], upto(b, 48, 48))
                else:
                    wait(dve, m_in[3], 48, b - 1, 48)
                src = max_bank(g)[0:16, 0:P]
                dve.tensor_scalar(m_parts[:, 0, :], src, -1.0, None, ALU.mult).then_inc(m_step, 1)
                dve.wait_ge(m_step, upto(b, 16, 4 * g + 1))
                dve.scalar_tensor_tensor(out=m_rest[:], in0=src, scalar=-1.0, in1=m_parts[:, 0, :],
                                         op0=ALU.mult, op1=ALU.subtract).then_inc(m_step, 1)
                dve.wait_ge(m_step, upto(b, 16, 4 * g + 2))
                dve.tensor_copy(m_parts[:, 1, :], m_rest[:]).then_inc(m_step, 1)
                dve.wait_ge(m_step, upto(b, 16, 4 * g + 3))
                dve.tensor_tensor(m_parts[:, 2, :], m_rest[:], m_parts[:, 1, :], ALU.subtract).then_inc(m_step, 1)

            def y_reciprocal(b, c):
                for g in (2 * c, 2 * c + 1):
                    dve.wait_ge(y_in[g], upto(b, 32, 32))
                v = denom[32 * c:32 * c + 32, :]
                dve.reciprocal(v, v).then_inc(y_rec, 1)

            def iteration(t, par):
                for slot in range(SLOTS):
                    b = t + 1
                    if slot - 1 in XT_SLOT and present(b):
                        n = XT_SLOT[slot - 1]
                        dve.wait_ge(xt_hi, upto(b, 2, n + 1))
                        wait(dve, qk_mm, 4, b - 1, 4)
                        dve.tensor_tensor(xT_lo[:, n, :], front_bank[:], xT_hi[:, n, :],
                                          ALU.subtract).then_inc(xt_lo, 1)
                    if slot - 1 in QK_SLOT and present(b):
                        n = QK_SLOT[slot - 1]
                        dve.wait_ge(qk_hi, upto(b, 4, n + 1))
                        wait(dve, qk_lo, 4, b, n) if n else wait(dve, qk_lo, 4, b - 1, 4)
                        dve.tensor_tensor(qk_rest[:], front_bank[:], parts[:, n % 2, 0, :],
                                          ALU.subtract).then_inc(qk_r, 1)
                    b = t - 1
                    if slot - 1 in PROJ_SLOT and present(b):
                        n = PROJ_SLOT[slot - 1]
                        dve.wait_ge(pr_mm, upto(b, 2, n + 1))
                        dve.wait_ge(res_in, upto(b, 16, 16))
                        r = res[:, 1 - par, 2 * n:2 * n + 2, :]
                        dve.tensor_tensor(r, proj_bank[n][:].rearrange("p (j c) -> p j c", c=C), r,
                                          ALU.add).then_inc(res_add, 1)
                    if slot - 1 in MAX_SLOT:
                        g = MAX_SLOT[slot - 1]
                        mb = t if g < 4 else t + 1
                        if present(mb):
                            max_split(mb, g % 4)
                    max_unit(t, par, slot)
                    if slot in INV_SLOT:
                        c = INV_SLOT[slot]
                        if present(t - c):
                            y_reciprocal(t - c, c)
                    if slot - NORM2_LAG in PROJ_SLOT and present(b):
                        n = PROJ_SLOT[slot - NORM2_LAG]
                        normalise(res[:, 1 - par], 1, (2 * n, 2 * n + 1), b, ln2_done)
                    if slot - STAT2_LAG in PROJ_SLOT and present(b):
                        n = PROJ_SLOT[slot - STAT2_LAG]
                        dve.wait_ge(res_add, upto(b, 2, n + 1))
                        statistics(res[:, 1 - par], 1, (2 * n, 2 * n + 1), b, 4 * n)
                    if slot in LN1_SLOT and present(t + 2):
                        normalise(emb[:, par], 0, LN1_SLOT[slot], t + 2, ln1_done)
                    if slot - 1 in X2T_SLOT and present(b):
                        n = X2T_SLOT[slot - 1]
                        dve.wait_ge(x2t_hi, upto(b, 2, n + 1))
                        wait(dve, f1_mm, 8, b - 1, 4 * n + 4)
                        cols = slice(256 * n, 256 * n + 256)
                        dve.tensor_tensor(x2T_lo[:, :, cols], x2t_bank[n][:].rearrange("p (c q) -> p c q", c=CC),
                                          x2T_hi[:, :, cols], ALU.subtract).then_inc(x2t_lo, 1)
                    n = OUT_ADD_SLOT.get(slot, 0)
                    b, bp = (t - 1 - n, 1 - par if n == 0 else par)
                    if slot in OUT_ADD_SLOT and present(b):
                        dve.wait_ge(f2_mm, upto(b, 8, 4 * n + 4))
                        dve.wait_ge(b2_add, upto(b, 4, 2 * n + 2))
                        r = res[:, bp, 2 * n:2 * n + 2, :]
                        dve.tensor_tensor(r, acc_bank[:].rearrange("p (j c) -> p j c", c=C), r,
                                          ALU.add).then_inc(out_add, 1)
                    if slot in LN1_STAT_SLOT and present(t + 2):
                        n = LN1_STAT_SLOT[slot]
                        wait(dve, emb_in, 64, t + 2, 64)
                        statistics(emb[:, par], 0, (2 * n, 2 * n + 1), t + 2, 4 * n)

            dve.wait_ge(const_ok, 6)
            steps = [0]

            def link(ins):
                steps[0] += 1
                ins.then_inc(w_step, 1)
                dve.wait_ge(w_step, steps[0])

            def chunk(n):
                dve.wait_ge(w_mm, n + 1 if n < ATTN_CHUNKS else n + 2)
                return w_bank[n % 4][:].rearrange("p (c f) -> p c f", c=2)

            def evacuated(n):
                assert steps[0] == W_EVACUATED[n], (n, steps[0])

            for k in range(3):
                src = chunk(k)
                if k == 2:
                    link(dve.tensor_copy(wv_hi[:], src))
                    link(dve.tensor_tensor(wv_lo[:], src, wv_hi[:], ALU.subtract))
                    evacuated(k)
                    continue
                scale = D ** -0.5 if k == 0 else 1.0
                for c in range(CC):
                    for half in range(2):
                        s = src[:, c, P * half:P * half + P].rearrange("p (h d) -> p h d", h=8)
                        n = 2 * half + k
                        hi = wqk_hi[:, c, n, :].rearrange("p (d h) -> p h d", h=8)
                        lo = wqk_lo[:, c, n, :].rearrange("p (d h) -> p h d", h=8)
                        link(dve.tensor_scalar(hi, s, scale, None, ALU.mult))
                        link(dve.scalar_tensor_tensor(out=lo, in0=s, scalar=scale, in1=hi, op0=ALU.mult,
                                                      op1=ALU.subtract))
                evacuated(k)
            link(dve.tensor_copy(wp[:], chunk(3)))
            evacuated(3)
            dve.wait_ge(emb_in, 64)
            for n in range(2):
                statistics(emb[:, 0], 0, (2 * n, 2 * n + 1), 0, 4 * n)
            dve.wait_ge(ffn_w_in, 32)
            for n, raw in enumerate((raw_w1, raw_w2)):
                link(dve.tensor_reduce(w_sum[:, n:n + 1], raw, AX.X, ALU.add, apply_absolute_value=True))
            assert steps[0] == W_SUMMED
            normalise(emb[:, 0], 0, range(NT), 0, ln1_done)
            dve.wait_ge(w_mm, ATTN_CHUNKS + 1)
            link(dve.tensor_scalar(w_thr[:, 0:2], acc_bank[:, 0:2], 1.0 / (FF * C), EPS, ALU.mult, ALU.add))
            link(dve.tensor_scalar(w_thr[:, 2:4], w_thr[:, 0:2], -0.5, None, ALU.mult))
            link(dve.tensor_scalar(w_thr[:, 0:2], w_thr[:, 0:2], 0.5, None, ALU.mult))
            for n, raw in enumerate((raw_w1, raw_w2)):
                for half in range(2):
                    w = raw[:, FC * P * half:FC * P * half + FC * P]
                    link(dve.tensor_scalar(below, w, w_thr[:, 2 + n:3 + n], None, ALU.is_lt))
                    link(dve.scalar_tensor_tensor(out=w, in0=w, scalar=w_thr[:, n:n + 1], in1=below,
                                                  op0=ALU.is_gt, op1=ALU.subtract))
                assert steps[0] == W_TERNARY[n]
            for k in range(FC // 2):
                link(dve.tensor_copy(w1T[:, :, 256 * k:256 * k + 256], chunk(4 + k)))
                evacuated(4 + k)
            for k in range(FC // 2):
                link(dve.tensor_copy(w2T[:, 2 * k:2 * k + 2, :], chunk(8 + k)))
                evacuated(8 + k)
            dve.drain().then_inc(w_ready, 1)

            schedule(dve, iteration)

        @block.tensor
        def _(pe):
            w1q = raw_w1.rearrange("p (j c) -> p j c", c=C)
            w2q = raw_w2.rearrange("p (j c) -> p j c", c=FF)

            def chunk(n, pairs):
                if n >= 4:
                    pe.wait_ge(w_step, W_EVACUATED[n - 4])
                for k, src in enumerate(pairs):
                    ins = pe.transpose(w_bank[n % 4][:, P * k:P * k + P], src, ident[:])
                ins.then_inc(w_mm, 1)

            pe.wait_ge(ident_ok, 1)
            pe.wait_ge(attn_in, 32)
            for k in range(3):
                chunk(k, [raw_attn[:, 2 * k + i, P * c:P * c + P] for c in range(CC) for i in range(2)])
            chunk(3, [raw_proj[:, i, P * c:P * c + P] for c in range(CC) for i in range(2)])
            pe.wait_ge(const_ok, 6)
            pe.wait_ge(w_step, W_SUMMED)
            pe.matmul(acc_bank[:, 0:2], ones, w_sum[:], start=True, stop=True).then_inc(w_mm, 1)
            pe.wait_ge(w_step, W_TERNARY[0])
            for k in range(FC // 2):
                chunk(4 + k, [w1q[:, 2 * k + i, P * c:P * c + P] for c in range(CC) for i in range(2)])
            pe.wait_ge(w_step, W_TERNARY[1])
            for k in range(FC // 2):
                chunk(8 + k, [w2q[:, c, P * (2 * k + i):P * (2 * k + i) + P] for i in range(2) for c in range(CC)])
            pe.wait_ge(w_ready, 1)

            def front_bank_free(t, slot):
                at = [s for s, _, _ in FRONT_USES].index(slot)
                back = 0
                while True:
                    at -= 1
                    if at < 0:
                        at, back = len(FRONT_USES) - 1, back + 1
                    if back > 1:
                        return
                    _, kind, n = FRONT_USES[at]
                    b = front_batch(kind, n, t - back)
                    if present(b):
                        break
                if kind == "xt":
                    pe.wait_ge(xt_lo, upto(b, 2, n + 1))
                elif kind == "qk":
                    pe.wait_ge(qk_r, upto(b, 4, n + 1))
                elif kind == "v":
                    pe.wait_ge(v_ev, upto(b, 2, n + 1))
                else:
                    pe.wait_ge(m_step, upto(b, 16, 4 * (n % 4) + 2))

            def st_unit(b, par, n):
                g, m = n // UNITS, n % UNITS
                if m == 0:
                    pe.wait_ge(m_in[g], upto(b, 48, 48))
                if n >= 2:
                    pe.wait_ge(exp_done, upto(b, 40, n - 1))
                else:
                    wait(pe, exp_done, 40, b - 1, 39 + n)
                blocks = st_blocks(m)
                for i, (h, kb, col) in enumerate(blocks):
                    q0 = kb * P
                    for rows, a, z in ((K_DIAGONAL, q0, q0 + P), (K_SHIFTED, q0 + P, T)):
                        if a < z:
                            ins = pe.matmul(st_bank[n % 2][:, col + a - q0:col + z - q0],
                                            k_aug[0:rows, par, GH * g + h, q0:q0 + P],
                                            q_aug[0:rows, par, GH * g + h, a:z], start=True, stop=True)
                ins.then_inc(st_mm, 1)

            def s_unit(t, par, slot):
                b, n = score_unit(t, slot)
                if not present(b):
                    return
                bp = par if b is t else 1 - par
                g, m = n // UNITS, n % UNITS
                if isinstance(b, int) and b == 0 and n == 0:
                    pe.wait_ge(aug_const_in, 128)
                if m == 0 and g % 2 == 0:
                    pe.wait_ge(aug_in[g], upto(b, 48, 48))
                    pe.wait_ge(aug_in[g + 1], upto(b, 48, 48))
                if n >= 2:
                    pe.wait_ge(s_max, upto(b, 40, n - 1))
                else:
                    wait(pe, s_max, 40, b - 1, 39 + n)
                for i, (h, qb, col) in enumerate(s_blocks(m)):
                    w = (qb + 1) * P
                    ins = pe.matmul(s_bank[n % 2][:, col:col + w],
                                    q_aug[0:K_SCORES, bp, GH * g + h, qb * P:qb * P + P],
                                    k_aug[0:K_SCORES, bp, GH * g + h, 0:w], start=True, stop=True)
                ins.then_inc(s_mm, 1)

            def pv(b, par, g, part):
                pe.wait_ge(zero_done, upto(b, 40, UNITS * g + (4, 8, 10)[part]))
                if part == 0:
                    if g == 0:
                        pe.wait_ge(v_ev, upto(b, 2, 2))
                        wait(pe, y_ev, 4, b - 1, 4)
                    else:
                        pe.wait_ge(y_ev, upto(b, 4, g))
                for kb in ((0,), (1, 3), (2,))[part]:
                    q0 = kb * P
                    for h in range(GH):
                        unit, col = P_AT[h, kb]
                        ins = pe.matmul(pv_bank[32 * h:32 * h + 32, q0:T], v_aug[:, par, kb, GH * g + h, :],
                                        prob[:, unit, col:col + T - q0], start=(kb == 0), stop=(kb == 2))
                ins.then_inc(pv_mm, 1)

            def x_transpose(b, c):
                if c == 0:
                    pe.wait_ge(ln1_done, upto(b, 4, 4))
                for j in range(NT):
                    ins = pe.transpose(front_bank[:, P * j:P * j + P], xn[:, j, P * c:P * c + P], ident[:])
                ins.then_inc(xt_mm, 1)

            def qk_project(b, n):
                if n == 0:
                    pe.wait_ge(xt_lo, upto(b, 2, 2))
                terms = [(w, xx, c) for c in range(CC)
                         for w, xx in ((wqk_hi, xT_hi), (wqk_hi, xT_lo), (wqk_lo, xT_hi))]
                for i, (w, xx, c) in enumerate(terms):
                    ins = pe.matmul(front_bank[:], w[:, c, n, :], xx[:, c, :], start=(i == 0),
                                    stop=(i == len(terms) - 1))
                ins.then_inc(qk_mm, 1)

            def v_project(b, n):
                terms = [(w, xx, c) for c in range(CC)
                         for w, xx in ((wv_hi, xT_hi), (wv_hi, xT_lo), (wv_lo, xT_hi))]
                for j in range(2):
                    tok = slice(P * (2 * n + j), P * (2 * n + j) + P)
                    for i, (w, xx, c) in enumerate(terms):
                        ins = pe.matmul(front_bank[:, C * j:C * j + C], xx[:, c, tok], w[:, c, :], start=(i == 0),
                                        stop=(i == len(terms) - 1))
                ins.then_inc(v_mm, 1)

            def out_project(b, n):
                if n == 0:
                    pe.wait_ge(y_nrm, upto(b, 2, 2))
                    wait(pe, out_add, 2, b - 1, 2)
                    wait(pe, m_step, 16, b + 1, 4 * 1 + 2)
                else:
                    wait(pe, f1_relu, 16, b - 1, 16)
                for j in range(2):
                    tok = slice(P * (2 * n + j), P * (2 * n + j) + P)
                    for c in range(CC):
                        ins = pe.matmul(proj_bank[n][:, C * j:C * j + C], yT[:, c, tok], wp[:, c, :],
                                        start=(c == 0), stop=(c == CC - 1))
                ins.then_inc(pr_mm, 1)

            def x2_transpose(b, n):
                pe.wait_ge(ln2_done, upto(b, 4, 2 * n + 2))
                if n == 0:
                    pe.wait_ge(res_add, upto(b, 2, 2))
                else:
                    wait(pe, m_step, 16, b + 1, 4 * 2 + 2)
                    pe.wait_ge(res_add, upto(b, 2, 1))
                for c in range(CC):
                    for j in range(2):
                        at = 256 * c + P * j
                        ins = pe.transpose(x2t_bank[n][:, at:at + P], xn[:, 2 * n + j, P * c:P * c + P], ident[:])
                ins.then_inc(x2t_mm, 1)

            def ffn_in(b, n):
                half, u = n // 4, n % 4
                pe.wait_ge(x2t_lo, upto(b, 2, half + 1))
                if n >= 1:
                    pe.wait_ge(f1_relu, upto(b, 16, 2 * n))
                for i in range(2):
                    f = 2 * u + i
                    terms = [(xx, c) for c in range(CC) for xx in (x2T_hi, x2T_lo)]
                    for k, (xx, c) in enumerate(terms):
                        ins = pe.matmul(ffn_bank[:, 256 * i:256 * i + 256], w1T[:, c, P * f:P * f + P],
                                        xx[:, c, 256 * half:256 * half + 256], start=(k == 0),
                                        stop=(k == len(terms) - 1))
                ins.then_inc(f1_mm, 1)

            def ffn_out(b, n):
                half, u = n // 4, n % 4
                pe.wait_ge(f1_lo, upto(b, 8, n + 1))
                if n == 0:
                    pe.wait_ge(x2t_lo, upto(b, 2, 2))
                elif n == 4:
                    pe.wait_ge(out_add, upto(b, 2, 1))
                for i in range(2):
                    f = 2 * u + i
                    for hh in (h_hi, h_lo):
                        for j in range(2):
                            first = u == 0 and i == 0 and hh is h_hi and j == 0
                            last = u == 3 and i == 1 and hh is h_lo
                            ins = pe.matmul(acc_bank[:, C * j:C * j + C], hh[:, f, P * j:P * j + P], w2T[:, f, :],
                                            start=first, stop=last, skip_group_check=True)
                ins.then_inc(f2_mm, 1)

            def iteration(t, par):
                for slot in range(SLOTS):
                    if present(t):
                        st_unit(t, par, slot)
                    s_unit(t, par, slot)
                    if slot % 10 in PV_SLOT:
                        part = PV_SLOT[slot % 10]
                        g = slot // 10 - (part > 0)
                        b, bp = (t, par) if g >= 0 else (t - 1, 1 - par)
                        if present(b):
                            pv(b, bp, g % 4, part)
                    b = t + 1
                    front = slot in XT_SLOT or slot in QK_SLOT or slot in V_SLOT
                    if front and present(b):
                        front_bank_free(t, slot)
                        if slot in XT_SLOT:
                            x_transpose(b, XT_SLOT[slot])
                        elif slot in QK_SLOT:
                            qk_project(b, QK_SLOT[slot])
                        else:
                            v_project(b, V_SLOT[slot])
                    if slot in MAX_SLOT:
                        g = MAX_SLOT[slot]
                        mb = t if g < 4 else t + 1
                        if present(mb):
                            if g not in OUT_BANK_GROUPS:
                                front_bank_free(t, slot)
                            elif g == 1:
                                wait(pe, out_add, 2, t - 2, 2)
                            else:
                                wait(pe, res_add, 2, t - 1, 1)
                            g %= 4
                            pe.wait_ge(s_max, upto(mb, 40, UNITS * g + UNITS))
                            pe.transpose(max_bank(g)[0:16, 0:P], row_max[:, g % 2, :], ident[:]).then_inc(m_mm, 1)
                    b = t - 1
                    if present(b):
                        if slot in PROJ_SLOT:
                            out_project(b, PROJ_SLOT[slot])
                        if slot in X2T_SLOT:
                            x2_transpose(b, X2T_SLOT[slot])
                        if slot in F1_SLOT:
                            ffn_in(b, F1_SLOT[slot])
                    if slot in F2_SLOT:
                        b = t - 1 if slot > min(X2T_SLOT) else t - 2
                        if present(b):
                            ffn_out(b, F2_SLOT[slot])

            schedule(pe, iteration)


def constants():
    bf = np.dtype("bfloat16")
    start = 2.0 ** (-8.0 / H)
    slopes = np.array([start ** (i + 1) for i in range(H)], np.float32)
    cut, rest = [], slopes.copy()
    for _ in range(3):
        p = rest.astype(bf)
        cut.append(p)
        rest = (rest - p.astype(np.float32)).astype(np.float32)
    pos = (np.arange(T) - T // 2).astype(bf)
    q = np.zeros((ALIBI_ROWS + SUB_ROWS, H, T), bf)
    k = np.zeros((ALIBI_ROWS + 3 + SUB_ROWS, H, T), bf)
    for i in range(3):
        q[i] = pos[None, :]
        k[i] = -cut[i][:, None]
        q[3 + i] = cut[i][:, None]
        k[3 + i] = pos[None, :]
    k[ALIBI_ROWS:ALIBI_ROWS + 3] = 1.0
    within = np.arange(T) % P
    for j in range(SUB_ROWS):
        q[ALIBI_ROWS + j] = np.where(within < SUB * (j + 1), MASKED, 0.0)[None, :]
        k[ALIBI_ROWS + 3 + j] = (within // SUB == j + 1)[None, :]
    return q.reshape(-1, H * T), k.reshape(-1, H * T)


def kernel(x, L0_tok_weight, L0_attn_W_attn, L0_attn_W_proj, L0_ffn_W1, L0_ffn_b1, L0_ffn_W2, L0_ffn_b2):
    import concourse.bacc as bacc
    from concourse.bass_utils import run_bass_kernel_spmd

    q_const, k_const = constants()
    given = {
        "x": x, "table": L0_tok_weight, "w_attn": L0_attn_W_attn, "w_proj": L0_attn_W_proj, "w1": L0_ffn_W1,
        "b1": L0_ffn_b1, "w2": L0_ffn_W2, "b2": L0_ffn_b2, "q_const": q_const, "k_const": k_const,
    }
    nc = bacc.Bacc("TRN2", target_bir_lowering=False, num_devices=1)
    arrays, args = {}, []
    for name, a in given.items():
        a = np.ascontiguousarray(a)
        arrays[name] = a
        args.append(nc.dram_tensor(name, a.shape, mybir.dt.from_np(a.dtype), kind="ExternalInput").ap())
    out = nc.dram_tensor("out", [NB * T, C], F32, kind="ExternalOutput").ap()
    block_program(nc, *args, out)
    r = run_bass_kernel_spmd(nc, [arrays], core_ids=[0])
    return r.results[0]["out"].reshape(NB, T, C)
```
